# Optimizing a Trainium2 kernel written in Bass

```python
import numpy as np
import jax
import jax.numpy as jnp

def _softmax(x, axis=-1):
    return jax.nn.softmax(x, axis=axis)
def _gelu(x):
    return jax.nn.gelu(x, approximate=True)
def _silu(x):
    return jax.nn.silu(x)
def _sigmoid(x):
    return jax.nn.sigmoid(x)
def _layernorm(x, axis=-1, eps=1e-5):
    m = jnp.mean(x, axis=axis, keepdims=True)
    v = jnp.var(x, axis=axis, keepdims=True)
    return (x - m) / jnp.sqrt(v + eps)
def _scatter_add(tgt, idx, src, axis=0):
    return tgt.at[idx].add(src)
def _segment_sum(src, seg, n):
    return jax.ops.segment_sum(src, seg, n)

kernel_name = 'mk_adj_preln_d4_adj_256_f06fb8'

def setup_inputs(seed: int = 0):
    np.random.seed(seed)
    _w = jnp.asarray
    def _rec_inputs():
        import jax
        import jax.numpy as jnp
        _gk = jax.random.key(seed)
        x = -0.0005207 + 1.001 * jax.random.normal(jax.random.fold_in(_gk, 1), (64, 256, 256), jnp.float32)
        _w = (1.0 + jnp.arange(256, dtype=jnp.float32)) ** -0.5
        _w = _w / _w.mean()
        _pij = jnp.clip(0.0625 * _w[:, None] * _w[None, :], 0.0, 1.0)
        _a = jax.random.uniform(jax.random.fold_in(_gk, 2), (64, 256, 256)) < _pij
        adj = _a.astype(jnp.int32)
        return x, adj
    x, adj = _rec_inputs()
    def _L0_gnn_setup():
        import jax, jax.numpy as jnp
        import numpy as np
        DIM = 256
        HEADS = 8
        HEAD_DIM = DIM // HEADS
        DFF = 4 * DIM
        EPS = 1e-05

        def _layernorm(x, g, b):
            m = jnp.mean(x, axis=-1, keepdims=True)
            v = jnp.mean(jnp.square(x - m), axis=-1, keepdims=True)
            return (x - m) * jax.lax.rsqrt(v + EPS) * g + b
        key = jax.random.key(seed)
        ks = jax.random.split(key, 12)
        B, N = (8, 1024)
        s = 1.0 / np.sqrt(DIM)
        x = jax.random.normal(ks[0], (B, N, DIM), dtype=jnp.float32)
        adj = jax.random.randint(ks[1], (B, N, N), 0, 2, dtype=jnp.int32)
        return {'x': x, 'adj': adj, 'Wqkv': jax.random.normal(ks[2], (3 * DIM, DIM), jnp.float32) * s, 'bqkv': jnp.zeros((3 * DIM,), jnp.float32), 'Wo': jax.random.normal(ks[3], (DIM, DIM), jnp.float32) * s, 'bo': jnp.zeros((DIM,), jnp.float32), 'ln1_g': jnp.ones((DIM,), jnp.float32), 'ln1_b': jnp.zeros((DIM,), jnp.float32), 'W1': jax.random.normal(ks[4], (DFF, DIM), jnp.float32) * s, 'b1': jnp.zeros((DFF,), jnp.float32), 'W2': jax.random.normal(ks[5], (DIM, DFF), jnp.float32) * (1.0 / np.sqrt(DFF)), 'b2': jnp.zeros((DIM,), jnp.float32), 'ln2_g': jnp.ones((DIM,), jnp.float32), 'ln2_b': jnp.zeros((DIM,), jnp.float32)}
    _L0_gnn_all = _L0_gnn_setup()
    _L0_gnn_in = {k: v for k, v in _L0_gnn_all.items() if k in ('Wqkv', 'bqkv', 'Wo', 'bo', 'ln1_g', 'ln1_b', 'W1', 'b1', 'W2', 'b2', 'ln2_g', 'ln2_b', )}
    del _L0_gnn_all

    def _L1_gnn_setup():
        import jax, jax.numpy as jnp
        import numpy as np
        key = jax.random.key(seed)
        k1, k2, k3, k4 = jax.random.split(key, 4)
        B, N, F, U = (8, 2048, 256, 256)
        x = jax.random.normal(k1, (B, N, F), dtype=jnp.float32)
        adj = jax.random.randint(k2, (B, N, N), 0, 2, dtype=jnp.int32)
        W_msg = jax.random.normal(k3, (F, U), dtype=jnp.float32) / np.sqrt(F)
        W_upd = jax.random.normal(k4, (F, U), dtype=jnp.float32) / np.sqrt(F)
        bias = jnp.zeros((U,), dtype=jnp.float32)
        return {'x': x, 'adj': adj, 'W_msg': W_msg, 'W_upd': W_upd, 'bias': bias}
    _L1_gnn_all = _L1_gnn_setup()
    _L1_gnn_in = {k: v for k, v in _L1_gnn_all.items() if k in ('W_msg', 'W_upd', 'bias', )}
    del _L1_gnn_all

    def _L2_gnn_setup():
        import jax, jax.numpy as jnp
        import numpy as np
        B, N, D = (8, 1024, 256)
        H, HO = (4, 64)
        T = 5
        NEG = -1000000000.0
        EPS = 1e-06
        key = jax.random.key(seed)
        ks = jax.random.split(key, 6)
        nodes_embed = jax.random.normal(ks[0], (B, N, D), dtype=jnp.float32)
        node_adj = jax.random.randint(ks[1], (B, N, N), 0, T + 1)
        W = jax.random.normal(ks[2], (H, D, HO), dtype=jnp.float32) * (1.0 / np.sqrt(D))
        a_src = jax.random.normal(ks[3], (H, T, HO), dtype=jnp.float32) * 0.1
        a_dst = jax.random.normal(ks[4], (H, T, HO), dtype=jnp.float32) * 0.1
        bias = jnp.zeros((H, HO), dtype=jnp.float32)
        ln_gamma = jnp.ones((H, HO), dtype=jnp.float32)
        ln_beta = jnp.zeros((H, HO), dtype=jnp.float32)
        return {'nodes_embed': nodes_embed, 'node_adj': node_adj, 'W': W, 'a_src': a_src, 'a_dst': a_dst, 'bias': bias, 'ln_gamma': ln_gamma, 'ln_beta': ln_beta}
    _L2_gnn_all = _L2_gnn_setup()
    _L2_gnn_in = {k: v for k, v in _L2_gnn_all.items() if k in ('W', 'a_src', 'a_dst', 'bias', 'ln_gamma', 'ln_beta', )}
    del _L2_gnn_all

    def _L3_gnn_setup():
        import jax, jax.numpy as jnp
        import numpy as np
        UNITS = 256
        NUM_HEADS = 8
        HEAD_DIM = UNITS // NUM_HEADS
        B, N = (8, 2048)
        key = jax.random.key(seed)
        ks = jax.random.split(key, 7)
        node_features = jax.random.normal(ks[0], (B, N, UNITS), dtype=jnp.float32)
        adjacency_matrix = jax.random.randint(ks[1], (B, N, N), 0, 2, dtype=jnp.int32)
        s = 1.0 / np.sqrt(UNITS)
        Wq = jax.random.normal(ks[2], (UNITS, UNITS), dtype=jnp.float32) * s
        Wk = jax.random.normal(ks[3], (UNITS, UNITS), dtype=jnp.float32) * s
        Wv = jax.random.normal(ks[4], (UNITS, UNITS), dtype=jnp.float32) * s
        Wo = jax.random.normal(ks[5], (UNITS, UNITS), dtype=jnp.float32) * s
        bo = jnp.zeros((UNITS,), dtype=jnp.float32)
        return {'node_features': node_features, 'adjacency_matrix': adjacency_matrix, 'Wq': Wq, 'Wk': Wk, 'Wv': Wv, 'Wo': Wo, 'bo': bo}
    _L3_gnn_all = _L3_gnn_setup()
    _L3_gnn_in = {k: v for k, v in _L3_gnn_all.items() if k in ('Wq', 'Wk', 'Wv', 'Wo', 'bo', )}
    del _L3_gnn_all

    return {
        "x": x,
        "adj": adj,
        "L0_gnn_Wqkv": _L0_gnn_in["Wqkv"],
        "L0_gnn_bqkv": _L0_gnn_in["bqkv"],
        "L0_gnn_Wo": _L0_gnn_in["Wo"],
        "L0_gnn_bo": _L0_gnn_in["bo"],
        "L0_gnn_ln1_g": _L0_gnn_in["ln1_g"],
        "L0_gnn_ln1_b": _L0_gnn_in["ln1_b"],
        "L0_gnn_W1": _L0_gnn_in["W1"],
        "L0_gnn_b1": _L0_gnn_in["b1"],
        "L0_gnn_W2": _L0_gnn_in["W2"],
        "L0_gnn_b2": _L0_gnn_in["b2"],
        "L0_gnn_ln2_g": _L0_gnn_in["ln2_g"],
        "L0_gnn_ln2_b": _L0_gnn_in["ln2_b"],
        "L1_gnn_W_msg": _L1_gnn_in["W_msg"],
        "L1_gnn_W_upd": _L1_gnn_in["W_upd"],
        "L1_gnn_bias": _L1_gnn_in["bias"],
        "L2_gnn_W": _L2_gnn_in["W"],
        "L2_gnn_a_src": _L2_gnn_in["a_src"],
        "L2_gnn_a_dst": _L2_gnn_in["a_dst"],
        "L2_gnn_bias": _L2_gnn_in["bias"],
        "L2_gnn_ln_gamma": _L2_gnn_in["ln_gamma"],
        "L2_gnn_ln_beta": _L2_gnn_in["ln_beta"],
        "L3_gnn_Wq": _L3_gnn_in["Wq"],
        "L3_gnn_Wk": _L3_gnn_in["Wk"],
        "L3_gnn_Wv": _L3_gnn_in["Wv"],
        "L3_gnn_Wo": _L3_gnn_in["Wo"],
        "L3_gnn_bo": _L3_gnn_in["bo"],
    }

def reference(x, adj, L0_gnn_Wqkv, L0_gnn_bqkv, L0_gnn_Wo, L0_gnn_bo, L0_gnn_ln1_g, L0_gnn_ln1_b, L0_gnn_W1, L0_gnn_b1, L0_gnn_W2, L0_gnn_b2, L0_gnn_ln2_g, L0_gnn_ln2_b, L1_gnn_W_msg, L1_gnn_W_upd, L1_gnn_bias, L2_gnn_W, L2_gnn_a_src, L2_gnn_a_dst, L2_gnn_bias, L2_gnn_ln_gamma, L2_gnn_ln_beta, L3_gnn_Wq, L3_gnn_Wk, L3_gnn_Wv, L3_gnn_Wo, L3_gnn_bo):
    import jax
    import jax.numpy as jnp
    def _L0_gnn_ref(x, adj, Wqkv, bqkv, Wo, bo, ln1_g, ln1_b, W1, b1, W2, b2, ln2_g, ln2_b):
        import jax, jax.numpy as jnp
        import numpy as np
        DIM = 256
        HEADS = 8
        HEAD_DIM = DIM // HEADS
        DFF = 4 * DIM
        EPS = 1e-05

        def _layernorm(x, g, b):
            m = jnp.mean(x, axis=-1, keepdims=True)
            v = jnp.mean(jnp.square(x - m), axis=-1, keepdims=True)
            return (x - m) * jax.lax.rsqrt(v + EPS) * g + b
        B, N, _ = x.shape
        eye = jnp.eye(N, dtype=bool)[None]
        allowed = (adj > 0) | (jnp.swapaxes(adj, 1, 2) > 0) | eye
        qkv = x @ Wqkv.T + bqkv
        q, k, v = jnp.split(qkv, 3, axis=-1)

        def heads(t):
            return t.reshape(B, N, HEADS, HEAD_DIM).transpose(0, 2, 1, 3)
        q, k, v = (heads(q), heads(k), heads(v))
        scale = 1.0 / np.sqrt(HEAD_DIM)
        scores = jnp.einsum('bhqd,bhkd->bhqk', q * scale, k)
        scores = jnp.where(allowed[:, None], scores, -jnp.inf)
        attn = jax.nn.softmax(scores, axis=-1)
        ctx = jnp.einsum('bhqk,bhkd->bhqd', attn, v)
        ctx = ctx.transpose(0, 2, 1, 3).reshape(B, N, DIM)
        attn_out = ctx @ Wo.T + bo
        x = _layernorm(x + attn_out, ln1_g, ln1_b)
        ff = jax.nn.relu(x @ W1.T + b1) @ W2.T + b2
        x = _layernorm(x + ff, ln2_g, ln2_b)
        return x

    def _L1_gnn_ref(x, adj, W_msg, W_upd, bias):
        import jax, jax.numpy as jnp
        import numpy as np
        a = adj.astype(x.dtype)
        h = jnp.einsum('bnf,fu->bnu', x, W_msg)
        msg_sum = jnp.einsum('bij,biu->bju', a, h)
        deg = jnp.sum(a, axis=1)
        messages = jnp.where(deg[..., None] > 0, msg_sum / jnp.maximum(deg, 1.0)[..., None], 0.0)
        out = jnp.einsum('bnf,fu->bnu', x, W_upd) + messages + bias
        return jax.nn.relu(out)

    def _L2_gnn_ref(nodes_embed, node_adj, W, a_src, a_dst, bias, ln_gamma, ln_beta):
        import jax, jax.numpy as jnp
        import numpy as np
        B, N, D = (8, 1024, 256)
        H, HO = (4, 64)
        T = 5
        NEG = -1000000000.0
        EPS = 1e-06
        h = jnp.einsum('bnd,hde->bhne', nodes_embed, W)
        e_src = jnp.einsum('bhne,hte->bhtn', h, a_src)
        e_dst = jnp.einsum('bhne,hte->bhtn', h, a_dst)
        n_types = a_src.shape[1]
        weight = jnp.zeros(h.shape[:2] + (h.shape[2], h.shape[2]), dtype=h.dtype)
        for t in range(n_types):
            mask = (node_adj == t + 1).astype(h.dtype)[:, None]
            weight = weight + mask * (e_src[:, :, t, :, None] + e_dst[:, :, t, None, :])
        weight = jax.nn.leaky_relu(weight, negative_slope=0.01)
        weight = jnp.where(node_adj[:, None] == 0, NEG, weight)
        attention = jax.nn.softmax(weight, axis=-1)
        dst = jnp.einsum('bhij,bhje->bhie', attention, h) + bias[None, :, None, :]
        out = jax.nn.relu(dst) + h
        mu = out.mean(axis=-1, keepdims=True)
        var = out.var(axis=-1, keepdims=True)
        out = (out - mu) / jnp.sqrt(var + EPS) * ln_gamma[None, :, None, :] + ln_beta[None, :, None, :]
        b, hh, n, e = out.shape
        return out.transpose(0, 2, 1, 3).reshape(b, n, hh * e)

    def _L3_gnn_ref(node_features, adjacency_matrix, Wq, Wk, Wv, Wo, bo):
        import jax, jax.numpy as jnp
        import numpy as np
        UNITS = 256
        NUM_HEADS = 8
        HEAD_DIM = UNITS // NUM_HEADS
        B, N = (8, 2048)
        b, n, _ = node_features.shape
        h, d = (NUM_HEADS, HEAD_DIM)
        q = (node_features @ Wq).reshape(b, n, h, d).transpose(0, 2, 1, 3)
        k = (node_features @ Wk).reshape(b, n, h, d).transpose(0, 2, 1, 3)
        v = (node_features @ Wv).reshape(b, n, h, d).transpose(0, 2, 1, 3)
        scores = jnp.einsum('bhqd,bhkd->bhqk', q, k) / jnp.sqrt(jnp.float32(d))
        mask = adjacency_matrix[:, None, :, :] > 0
        scores = jnp.where(mask, scores, jnp.float32(-1000000000.0))
        w = jax.nn.softmax(scores, axis=-1)
        ctx = jnp.einsum('bhqk,bhkd->bhqd', w, v)
        ctx = ctx.transpose(0, 2, 1, 3).reshape(b, n, h * d)
        return ctx @ Wo + bo

    h = jnp.maximum(_layernorm(x, axis=-1), 0.0)
    x = x + _L0_gnn_ref(h, adj, L0_gnn_Wqkv, L0_gnn_bqkv, L0_gnn_Wo, L0_gnn_bo, L0_gnn_ln1_g, L0_gnn_ln1_b, L0_gnn_W1, L0_gnn_b1, L0_gnn_W2, L0_gnn_b2, L0_gnn_ln2_g, L0_gnn_ln2_b)
    h = jnp.maximum(_layernorm(x, axis=-1), 0.0)
    x = x + _L1_gnn_ref(h, adj, L1_gnn_W_msg, L1_gnn_W_upd, L1_gnn_bias)
    h = jnp.maximum(_layernorm(x, axis=-1), 0.0)
    x = x + _L2_gnn_ref(h, adj, L2_gnn_W, L2_gnn_a_src, L2_gnn_a_dst, L2_gnn_bias, L2_gnn_ln_gamma, L2_gnn_ln_beta)
    h = jnp.maximum(_layernorm(x, axis=-1), 0.0)
    x = x + _L3_gnn_ref(h, adj, L3_gnn_Wq, L3_gnn_Wk, L3_gnn_Wv, L3_gnn_Wo, L3_gnn_bo)
    return x


_drawn_inputs = setup_inputs


def setup_inputs(seed=0):
    import zlib

    import numpy as np

    out = dict(_drawn_inputs(seed))
    spreads = {'L0_gnn_bqkv': (0.0, 0.1),
     'L0_gnn_bo': (0.0, 0.1),
     'L0_gnn_ln1_g': (1.0, 0.2),
     'L0_gnn_ln1_b': (0.0, 0.1),
     'L0_gnn_b1': (0.0, 0.271),
     'L0_gnn_b2': (0.0, 0.1),
     'L0_gnn_ln2_g': (1.0, 0.2),
     'L0_gnn_ln2_b': (0.0, 0.1),
     'L1_gnn_bias': (0.0, 0.1),
     'L2_gnn_bias': (0.0, 0.1),
     'L2_gnn_ln_gamma': (1.0, 0.2),
     'L2_gnn_ln_beta': (0.0, 0.1),
     'L3_gnn_bo': (0.0, 0.1)}
    factors = {'L2_gnn_a_src': 4.264}
    for name, (base, spread) in spreads.items():
        noise = np.random.default_rng([zlib.crc32(name.encode()), seed]).standard_normal(out[name].shape)
        drawn = base * np.exp(spread * noise) if base else spread * noise
        out[name] = jnp.asarray(drawn.astype(out[name].dtype))
    for name, factor in factors.items():
        out[name] = (out[name] * factor).astype(out[name].dtype)
    return out
```

```python
from contextlib import ExitStack

import numpy as np

import concourse.bass as bass
from concourse import mybir

ALU = mybir.AluOpType
ACT = mybir.ActivationFunctionType
AX = mybir.AxisListType
F32 = mybir.dt.float32
BF16 = mybir.dt.bfloat16
I32 = mybir.dt.int32

P = 128
N = 256
D = 256
NT = N // P
KT = D // P
HEADS, HD = 8, 32
H2, HO = 4, 64
TYPES = 5
FF = 1024
FT = FF // P
SLOTS = 2
MASKED = -float(2 ** 100)
EPS_L0, EPS_PRE, EPS_L2 = 1e-5, 1e-5, 1e-6
QSCALE = float(np.float32(1.0 / np.sqrt(HD)))

ROWS = ["bv", "bo0", "ln1_g", "ln1_b", "b2", "ln2_g", "ln2_b", "l1_bias", "l2_g", "l2_b", "bo3"]
COLS = {"bq": (0, 2), "bk": (2, 2), "ln1_g": (4, 2), "ln1_b": (6, 2), "b1": (8, FT), "l2_bias": (8 + FT, 2)}
NCOLS = 10 + FT

PRE0, POST1, POST2, PRE1, PRE2, PRE3 = range(6)
TRANSPOSED = {PRE0: 0, POST1: 1, PRE1: 2, PRE2: 3, PRE3: 4}
HT_DONE = {PRE0: 1, POST1: 3, PRE1: 4, PRE2: 5, PRE3: 6}
ATTN = {0: (0, HEADS), 2: (HEADS, H2), 3: (HEADS + H2, HEADS)}
ATTN_NO = {0: 0, 2: 1, 3: 2}
ALL_HEADS = 2 * HEADS + H2

PER_GRAPH = {
    "x_loaded": 16, "adj_loaded": 16, "out_stored": 16,
    "adjf_ready": 1, "adjT_psum": 1, "adjT_ready": 1, "mask0_step": 2, "mask0_ready": 1, "mask3_ready": 1,
    "mask2_ready": 1, "types_ready": 2 * TYPES,
    "ln_stats": 2 * 6, "ln_aggr": 2 * 6, "ln_var": 6, "ln_rstd": 6, "ln_z": 2 * 6, "zT_psum": 5, "hT_ready": 6,
    "q_psum": 2, "k_psum": 2, "v_psum": 2, "q_ready": 3, "k_ready": 3, "v_ready": 4,
    "s_psum": ALL_HEADS, "negmax": ALL_HEADS, "probs": 2 * ALL_HEADS, "pT_psum": ALL_HEADS, "pT_ready": ALL_HEADS,
    "pv_done": ALL_HEADS,
    "rinv": 3, "rwide": 3, "rT_psum": 3, "rT_ready": 3, "ctxT_ready": 3,
    "hb_ready": 2, "wo_psum": 2, "r1_ready": 1, "r1n_ready": 2, "ff1_psum": 4, "ff_act": 4, "ff_dve": 4,
    "ff2_psum": 1, "r2_ready": 1, "xplus": 1, "xa_step": 1, "xa_ready": 1,
    "l1_psum": 2, "hm_ready": 2, "upd_ready": 2, "msg_psum": 2, "deg_step": 6, "msg_ready": 2, "xb_ready": 1,
    "l2_psum": 2, "h2_ready": 2, "e_ready": 2, "uw": 4 * TYPES * H2, "z_sum": H2, "z_leaky": H2,
    "c2_ready": 2, "c2_psum": 1, "o2_ready": 1, "hln_stats": 8, "hln_aggr": 8, "hln_var": 1, "hln_rstd": 1,
    "o2_step": 2, "xc_step": 2, "xc_ready": 1, "xc_bo": 1, "out_ready": 1,
}

PRIMED = ["adjf_ready", "xplus", "ln_z", "msg_psum", "adjT_psum", "r1_ready", "r2_ready", "s_psum", "uw", "xa_ready",
          "xb_ready", "xc_bo", "out_ready", "mask2_ready", "types_ready", "out_stored"]


def build(nc, x, adj, wqkv0, wo0, w1, w2, wl1, wl2, w2t, ablk, wqkv3, wo3, rows, cols, out):
    graphs = x.shape[0]
    rounds = graphs // SLOTS
    x_v = x.rearrange("g (t p) f -> g p t f", p=P)
    adj_v = adj.rearrange("g (t p) f -> g p t f", p=P)
    out_v = out.rearrange("g (t p) f -> g p t f", p=P)
    EC = 2 * H2 * TYPES

    with ExitStack() as ctx:
        def sb(name, shape, dt=F32):
            return ctx.enter_context(nc.sbuf_tensor(name, shape, dt))

        def slots(name, shape, dt=F32):
            return [sb(f"{name}{s}", shape, dt) for s in range(SLOTS)]

        wqkv0_s = sb("wqkv0_s", [P, KT, 3 * D])
        wo0_s = sb("wo0_s", [P, KT, D])
        w1_s = sb("w1_s", [P, KT, FF])
        w2_s = sb("w2_s", [P, FT, D])
        wl1_s = sb("wl1_s", [P, KT, 2 * D])
        wl2_s = sb("wl2_s", [P, KT, D + EC])
        ablk_s = sb("ablk_s", [P, KT, EC])
        wqkv3_s = sb("wqkv3_s", [P, KT, 3 * D])
        wo3_s = sb("wo3_s", [P, KT, D])
        rows_s = sb("rows_s", [P, len(ROWS), D])
        cols_s = sb("cols_s", [P, NCOLS])
        lnb2 = sb("lnb2", [P, D])
        ident = sb("ident", [P, P])
        identb = sb("identb", [P, P], BF16)
        eye = sb("eye", [P, NT, N], BF16)
        power = sb("power", [P, 8])

        xin, adji = slots("xin", [P, NT, D]), slots("adji", [P, NT, N], I32)
        adjf = slots("adjf", [P, NT, N])
        mask0, mask3 = slots("mask0", [P, NT, N], BF16), slots("mask3", [P, NT, N], BF16)
        mask2 = slots("mask2", [P, NT, N], BF16)
        typ, typT = slots("typ", [P, TYPES, NT, N], BF16), slots("typT", [P, TYPES, NT, N], BF16)
        st, mv, var = slots("st", [P, NT, 6]), slots("mv", [P, NT, 2]), slots("var", [P, NT])
        rstd = slots("rstd", [P, NT])
        z, hT = slots("z", [P, NT, D]), slots("hT", [P, KT, N])
        qT, kT = slots("qT", [P, 2, N]), slots("kT", [P, 2, N])
        VW = HEADS * P + 96
        vp = slots("vp", [P, NT, VW])
        VW2 = H2 * P + 64
        vp2 = slots("vp2", [P, NT, VW2])
        nmax = slots("nmax", [P, 2, NT])
        pr, pT = slots("pr", [P, 2, NT, N]), slots("pT", [P, 2, NT, N])
        rsum, rinv = slots("rsum", [P, NT, HEADS]), slots("rinv", [P, NT, HEADS])
        rwide, rT, ctxT = slots("rwide", [P, NT, D]), slots("rT", [P, KT, N]), slots("ctxT", [P, KT, N])
        r1 = slots("r1", [P, NT, D])
        ffT = slots("ffT", [P, FT, N])
        xa, xb, xc = (slots(n, [P, NT, D]) for n in ("xa", "xb", "xc"))
        hm = slots("hm", [P, NT, D + 1])
        deg = slots("deg", [P, NT, 3])
        esd = slots("esd", [P, NT, EC])
        hst, hmv = slots("hst", [P, 8, 6]), slots("hmv", [P, 8, 2])
        hvar, hrs = slots("hvar", [P, 8]), slots("hrs", [P, 8])
        xo = slots("xo", [P, NT, D])

        adjT = [m[:, 0:NT, :] for m in ffT]
        ww = [m[:, 0:4, :].rearrange("p (a t) n -> p a t n", a=2) for m in ffT]
        uu = [m[:, 4:8, :].rearrange("p (a t) n -> p a t n", a=2) for m in ffT]
        mtmp = zs = rT
        hb = upd = o2 = r1
        r1n = rwide
        zl = [[z[s], rwide[s]] for s in range(SLOTS)]
        xplus = xb
        w2t_s = pT[0][:, 0]

        bank = [[ctx.enter_context(nc.psum_tensor(f"bank{s}{b}", [P, 2, 256], F32)) for b in range(4)]
                for s in range(SLOTS)]

        sems = {n: [ctx.enter_context(nc.semaphore(f"{n}{s}")) for s in range(SLOTS)] for n in PER_GRAPH}
        weights_loaded = ctx.enter_context(nc.semaphore("weights_loaded"))
        consts_set = ctx.enter_context(nc.semaphore("consts_set"))
        zeros_set = ctx.enter_context(nc.semaphore("zeros_set"))
        eye_ready = ctx.enter_context(nc.semaphore("eye_ready"))
        wait_carried = ctx.enter_context(nc.semaphore("wait_carried"))
        wa_psum = ctx.enter_context(nc.semaphore("wa_psum"))
        wa_ready = ctx.enter_context(nc.semaphore("wa_ready"))

        def row(name):
            return rows_s[:, ROWS.index(name), :]

        def rowt(name):
            r = ROWS.index(name)
            return rows_s[:, r:r + 1, :].broadcast_to([P, NT, D])

        def col(name, k):
            c = COLS[name][0] + k
            return cols_s[:, c:c + 1]

        def sem(name, s):
            return sems[name][s]

        def nth(name, i, k):
            return i * PER_GRAPH[name] + (k if name in PRIMED else k - PER_GRAPH[name])

        def past(name, i):
            assert name in PRIMED
            return i * PER_GRAPH[name]

        def head_window(s, layer, h, t):
            if layer == 2:
                a = h * P + 64 - HO * (h % 2)
                return vp2[s][:, t, a:a + P]
            a = h * P + 96 - HD * (h % 4)
            return vp[s][:, t, a:a + P]

        STEPS = []

        def both(*step):
            STEPS.extend((s, *step) for s in range(SLOTS))

        def attention(layer):
            n = ATTN[layer][1]
            for k in range(n + 2):
                if k < n:
                    both("scores", layer, k)
                if 1 <= k <= n:
                    both("turn", layer, k - 1)
                if k >= 2:
                    both("weigh", layer, k - 2)
            both("normal", layer)

        both("prepare")
        both("norm", PRE0)
        both("masks")
        both("qkv", 0)
        attention(0)
        both("attn_out", 0)
        both("norm", POST1)
        both("ff")
        both("norm", POST2)
        both("add0")
        both("norm", PRE1)
        both("mean_step")
        both("norm", PRE2)
        both("types_in")
        attention(2)
        both("types_out")
        both("norm", PRE3)
        both("qkv", 3)
        attention(3)
        both("attn_out", 3)

        ln_src = {PRE0: ("x_loaded", 16, xin), POST1: ("r1_ready", 1, r1), POST2: ("r2_ready", 1, r1),
                  PRE1: ("xa_ready", 1, xa), PRE2: ("xb_ready", 1, xb), PRE3: ("xc_ready", 1, xc)}

        block = ctx.enter_context(nc.Block())

        @block.sync
        def _(sp):
            for name in PRIMED:
                for s in range(SLOTS):
                    sp.sem_inc(sem(name, s), PER_GRAPH[name])
            for dst, src in ((wqkv0_s, wqkv0), (wo0_s, wo0), (w1_s, w1), (w2_s, w2), (wl1_s, wl1),
                             (w2t_s, w2t), (ablk_s, ablk), (wqkv3_s, wqkv3), (wo3_s, wo3)):
                sp.dma_start(dst[:] if dst is not w2t_s else dst, src.rearrange("(t p) n -> p t n", p=P)).then_inc(weights_loaded, 16)
            sp.dma_start(wl2_s[:, :, 0:D], wl2.rearrange("(t p) n -> p t n", p=P)).then_inc(weights_loaded, 16)
            sp.dma_start(rows_s[:], rows).then_inc(weights_loaded, 16)
            sp.dma_start(cols_s[:], cols).then_inc(weights_loaded, 16)
            with sp.Fori(1, rounds + 1) as i:
                for s in range(SLOTS):
                    sp.wait_ge(sem("adjf_ready", s), past("adjf_ready", i))
                    sp.sem_inc(wait_carried, 1)
                    sp.dma_start(adji[s][:], adj_v[i * SLOTS + (s - SLOTS)]).then_inc(sem("adj_loaded", s), 16)
                    sp.wait_ge(sem("xplus", s), past("xplus", i))
                    sp.sem_inc(wait_carried, 1)
                    sp.wait_ge(sem("ln_z", s), past("ln_z", i))
                    sp.sem_inc(wait_carried, 1)
                    sp.dma_start(xin[s][:], x_v[i * SLOTS + (s - SLOTS)]).then_inc(sem("x_loaded", s), 16)
                for s in range(SLOTS):
                    sp.wait_ge(sem("out_ready", s), nth("out_ready", i, 1))
                    sp.sem_inc(wait_carried, 1)
                    sp.dma_start(out_v[i * SLOTS + (s - SLOTS)], xo[s][:]).then_inc(sem("out_stored", s), 16)
            for s in range(SLOTS):
                sp.wait_ge(sem("out_stored", s), 16 * (rounds + 1))

        @block.gpsimd
        def _(pool):
            nc.gpsimd.memset(power[:], -0.5).then_inc(consts_set, 1)
            nc.gpsimd.memset(ident[:], 0.0).then_inc(consts_set, 1)
            nc.gpsimd.memset(identb[:], 0.0).then_inc(consts_set, 1)
            nc.gpsimd.memset(eye[:], 0.0).then_inc(consts_set, 1)
            pool.wait_ge(consts_set, 4)
            for m in (ident, identb):
                nc.gpsimd.affine_select(out=m[:], in_=m[:], compare_op=ALU.not_equal, fill=1.0, base=0,
                                        pattern=[[-1, P]], channel_multiplier=1).then_inc(eye_ready, 1)
            for t in range(NT):
                nc.gpsimd.affine_select(out=eye[:, t, :], in_=eye[:, t, :], compare_op=ALU.not_equal, fill=1.0,
                                        base=t * P, pattern=[[-1, N]], channel_multiplier=1).then_inc(eye_ready, 1)
            pool.wait_ge(weights_loaded, 16 * 12)
            nc.gpsimd.tensor_tensor(lnb2[:], row("ln1_b"), row("b2"), ALU.add).then_inc(eye_ready, 1)
            pool.wait_ge(eye_ready, 5)

            def powered(i, s, eps, src, tmp, dst, steps, done, n, k):
                nc.gpsimd.tensor_scalar(tmp, src, eps, None, ALU.add).then_inc(sem(steps, s), 1)
                pool.wait_ge(sem(steps, s), nth(steps, i, k + 1))
                pool.sem_inc(wait_carried, 1)
                nc.gpsimd.tensor_tensor(dst, tmp, power[:, 0:n], ALU.pow).then_inc(sem(done, s), 1)

            with pool.Fori(1, rounds + 1) as i:
                for s, what, *arg in STEPS:
                    if what == "prepare":
                        pool.wait_ge(sem("adj_loaded", s), nth("adj_loaded", i, 16))
                        pool.sem_inc(wait_carried, 1)
                        pool.wait_ge(sem("msg_psum", s), past("msg_psum", i))
                        pool.sem_inc(wait_carried, 1)
                        pool.wait_ge(sem("adjT_psum", s), past("adjT_psum", i))
                        pool.sem_inc(wait_carried, 1)
                        nc.gpsimd.tensor_copy(adjf[s][:], adji[s][:]).then_inc(sem("adjf_ready", s), 1)
                    if what == "norm":
                        ln = arg[0]
                        pool.wait_ge(sem("ln_aggr", s), nth("ln_aggr", i, 2 * ln + 2))
                        pool.sem_inc(wait_carried, 1)
                        powered(i, s, EPS_PRE, mv[s][:, :, 1], var[s][:], rstd[s][:], "ln_var", "ln_rstd", NT, ln)
                        if ln == PRE0:
                            pool.wait_ge(sem("ln_z", s), nth("ln_z", i, 2))
                            pool.sem_inc(wait_carried, 1)
                            pool.wait_ge(sem("r1_ready", s), past("r1_ready", i))
                            pool.sem_inc(wait_carried, 1)
                            nc.gpsimd.tensor_scalar(hb[s][:], z[s][:], 0.0, None, ALU.max).then_inc(sem("hb_ready", s), 1)
                            pool.wait_ge(sem("hb_ready", s), nth("hb_ready", i, 1))
                            pool.sem_inc(wait_carried, 1)
                            nc.gpsimd.tensor_tensor(hb[s][:], hb[s][:], rowt("bo0"), ALU.add)\
                                .then_inc(sem("hb_ready", s), 1)
                        if ln == POST1:
                            pool.wait_ge(sem("ln_z", s), nth("ln_z", i, 4))
                            pool.sem_inc(wait_carried, 1)
                            pool.wait_ge(sem("r2_ready", s), past("r2_ready", i))
                            pool.sem_inc(wait_carried, 1)
                            nc.gpsimd.tensor_tensor(r1n[s][:], z[s][:], rowt("ln1_g"), ALU.mult)\
                                .then_inc(sem("r1n_ready", s), 1)
                            pool.wait_ge(sem("r1n_ready", s), nth("r1n_ready", i, 1))
                            pool.sem_inc(wait_carried, 1)
                            nc.gpsimd.tensor_tensor(r1n[s][:], r1n[s][:], lnb2[:, None, :].broadcast_to([P, NT, D]), ALU.add)\
                                .then_inc(sem("r1n_ready", s), 1)
                    if what == "masks":
                        pool.wait_ge(sem("s_psum", s), past("s_psum", i))
                        pool.sem_inc(wait_carried, 1)
                        nc.gpsimd.tensor_scalar(mask3[s][:], adjf[s][:], 0.0, MASKED, ALU.is_le, ALU.mult)\
                            .then_inc(sem("mask3_ready", s), 1)
                        pool.wait_ge(sem("adjT_ready", s), nth("adjT_ready", i, 1))
                        pool.sem_inc(wait_carried, 1)
                        pool.wait_ge(sem("uw", s), past("uw", i))
                        pool.sem_inc(wait_carried, 1)
                        nc.gpsimd.tensor_scalar(mask2[s][:], adjT[s][:], 0.0, MASKED, ALU.is_equal, ALU.mult)\
                            .then_inc(sem("mask2_ready", s), 1)
                        for t in range(TYPES):
                            nc.gpsimd.tensor_scalar(typ[s][:, t], adjf[s][:], float(t + 1), None, ALU.is_equal)\
                                .then_inc(sem("types_ready", s), 1)
                            nc.gpsimd.tensor_scalar(typT[s][:, t], adjT[s][:], float(t + 1), None, ALU.is_equal)\
                                .then_inc(sem("types_ready", s), 1)
                        pool.wait_ge(sem("xa_ready", s), past("xa_ready", i))
                        pool.sem_inc(wait_carried, 1)
                        nc.gpsimd.tensor_tensor(xplus[s][:], xin[s][:], rowt("ln2_b"), ALU.add)\
                            .then_inc(sem("xplus", s), 1)
                    if what == "add0":
                        pool.wait_ge(sem("ln_z", s), nth("ln_z", i, 6))
                        pool.sem_inc(wait_carried, 1)
                        pool.wait_ge(sem("xb_ready", s), past("xb_ready", i))
                        pool.sem_inc(wait_carried, 1)
                        nc.gpsimd.tensor_tensor(xa[s][:], z[s][:], rowt("ln2_g"), ALU.mult).then_inc(sem("xa_step", s), 1)
                        pool.wait_ge(sem("xa_step", s), nth("xa_step", i, 1))
                        pool.sem_inc(wait_carried, 1)
                        pool.wait_ge(sem("xplus", s), nth("xplus", i, 1))
                        pool.sem_inc(wait_carried, 1)
                        nc.gpsimd.tensor_tensor(xa[s][:], xa[s][:], xplus[s][:], ALU.add).then_inc(sem("xa_ready", s), 1)
                    if what == "types_out":
                        pool.wait_ge(sem("hln_aggr", s), nth("hln_aggr", i, 8))
                        pool.sem_inc(wait_carried, 1)
                        powered(i, s, EPS_L2, hmv[s][:, :, 1], hvar[s][:], hrs[s][:], "hln_var", "hln_rstd", 8, 0)
                        pool.wait_ge(sem("o2_step", s), nth("o2_step", i, 2))
                        pool.sem_inc(wait_carried, 1)
                        pool.wait_ge(sem("xb_ready", s), nth("xb_ready", i, 1))
                        pool.sem_inc(wait_carried, 1)
                        pool.wait_ge(sem("xc_bo", s), past("xc_bo", i))
                        pool.sem_inc(wait_carried, 1)
                        nc.gpsimd.tensor_tensor(xc[s][:], o2[s][:], rowt("l2_g"), ALU.mult).then_inc(sem("xc_step", s), 1)
                        pool.wait_ge(sem("xc_step", s), nth("xc_step", i, 1))
                        pool.sem_inc(wait_carried, 1)
                        nc.gpsimd.tensor_tensor(xc[s][:], xc[s][:], rowt("l2_b"), ALU.add).then_inc(sem("xc_step", s), 1)
                        pool.wait_ge(sem("xc_step", s), nth("xc_step", i, 2))
                        pool.sem_inc(wait_carried, 1)
                        nc.gpsimd.tensor_tensor(xc[s][:], xc[s][:], xb[s][:], ALU.add).then_inc(sem("xc_ready", s), 1)
                    if what == "qkv" and arg[0] == 3:
                        pool.wait_ge(sem("ln_z", s), nth("ln_z", i, 12))
                        pool.sem_inc(wait_carried, 1)
                        pool.wait_ge(sem("xc_ready", s), nth("xc_ready", i, 1))
                        pool.sem_inc(wait_carried, 1)
                        nc.gpsimd.tensor_tensor(xc[s][:], xc[s][:], rowt("bo3"), ALU.add).then_inc(sem("xc_bo", s), 1)

        @block.scalar
        def _(act):
            act.wait_ge(weights_loaded, 16 * 12)
            act.wait_ge(wa_psum, 1)
            nc.scalar.activation(wl2_s[:, :, D:D + EC], bank[0][0][:, :, 0:EC], ACT.Copy).then_inc(wa_ready, 1)
            act.wait_ge(zeros_set, 6 * SLOTS)

            with act.Fori(1, rounds + 1) as i:
                for s, what, *arg in STEPS:
                    b = bank[s]
                    if what == "norm" and arg[0] in TRANSPOSED:
                        ln = arg[0]
                        act.wait_ge(sem("zT_psum", s), nth("zT_psum", i, TRANSPOSED[ln] + 1))
                        if ln == POST1:
                            for k in range(KT):
                                nc.scalar.activation(hT[s][:, k, :], b[2][:, k, :], ACT.Identity,
                                   bias=col("ln1_b", k), scale=col("ln1_g", k)).then_inc(sem("hT_ready", s), 1)
                        else:
                            nc.scalar.activation(hT[s][:], b[2][:], ACT.Relu).then_inc(sem("hT_ready", s), 1)
                    if what == "qkv":
                        act.wait_ge(sem("k_psum", s), nth("k_psum", i, 1 + (arg[0] == 3)))
                        if arg[0] == 0:
                            act.wait_ge(sem("s_psum", s), past("s_psum", i))
                            for k in range(2):
                                nc.scalar.activation(kT[s][:, k, :], b[1][:, k, :], ACT.Identity, bias=col("bk", k)).then_inc(sem("k_ready", s), 1)
                        else:
                            nc.scalar.activation(kT[s][:], b[1][:], ACT.Copy).then_inc(sem("k_ready", s), 1)
                            act.wait_ge(sem("v_psum", s), nth("v_psum", i, 2))
                            for t in range(NT):
                                nc.scalar.activation(vp[s][:, t, 96:VW].rearrange("p (h c) -> p h c", c=P)[:, :, 0:HD],
                                   b[3][:, t, :].rearrange("p (h d) -> p h d", d=HD), ACT.Copy).then_inc(sem("v_ready", s), 1)
                    if what == "turn":
                        layer, h = arg
                        a = ATTN[layer][0] + h
                        act.wait_ge(sem("negmax", s), nth("negmax", i, a + 1))
                        if layer == 2:
                            act.wait_ge(sem("z_leaky", s), nth("z_leaky", i, h + 1))
                        if a >= 2:
                            act.wait_ge(sem("pT_psum", s), nth("pT_psum", i, a - 1))
                        src = zl[s][a % 2][:] if layer == 2 else b[a % 2]
                        for t in range(NT):
                            nc.scalar.activation(pr[s][:, a % 2, t, :], src[:, t, :], ACT.Exp,
                               bias=nmax[s][:, a % 2, t:t + 1], accum_out=rsum[s][:, t, h:h + 1]).then_inc(sem("probs", s), 1)
                    if what == "weigh" and arg[0] == 2:
                        layer, h = arg
                        a = ATTN[layer][0] + h
                        act.wait_ge(sem("pT_psum", s), nth("pT_psum", i, a + 1))
                        act.wait_ge(sem("pv_done", s), nth("pv_done", i, a - 1))
                        nc.scalar.activation(pT[s][:, a % 2], b[2][:], ACT.Copy).then_inc(sem("pT_ready", s), 1)
                    if what == "normal":
                        n = ATTN_NO[arg[0]]
                        act.wait_ge(sem("rT_psum", s), nth("rT_psum", i, n + 1))
                        nc.scalar.activation(rT[s][:], b[2][:], ACT.Copy).then_inc(sem("rT_ready", s), 1)
                    if what == "ff":
                        for f in range(0, 4, 2):
                            act.wait_ge(sem("ff1_psum", s), nth("ff1_psum", i, f + 1))
                            for k in range(2):
                                nc.scalar.activation(ffT[s][:, 2 * f + k, :], b[f % 2][:, k, :], ACT.Relu,
                                   bias=col("b1", 2 * f + k)).then_inc(sem("ff_act", s), 1)
                    if what == "mean_step":
                        for t in range(NT):
                            act.wait_ge(sem("l1_psum", s), nth("l1_psum", i, t + 1))
                            nc.scalar.activation(hm[s][:, t, 0:D], b[t][:, 0, :], ACT.Copy).then_inc(sem("hm_ready", s), 1)
                    if what == "types_in":
                        for t in range(NT):
                            act.wait_ge(sem("l2_psum", s), nth("l2_psum", i, t + 1))
                            nc.scalar.activation(vp2[s][:, t, 64:VW2].rearrange("p (h c) -> p h c", c=P)[:, :, 0:HO],
                               b[t][:, 0, :].rearrange("p (h d) -> p h d", d=HO), ACT.Copy).then_inc(sem("h2_ready", s), 1)
                    if what == "types_out":
                        act.wait_ge(sem("ctxT_ready", s), nth("ctxT_ready", i, 2))
                        for k in range(KT):
                            nc.scalar.activation(rT[s][:, k, :], ctxT[s][:, k, :], ACT.Relu, bias=col("l2_bias", k)).then_inc(sem("c2_ready", s), 1)

        @block.tensor
        def _(pe):
            def mm(o, lhsT, rhs, start, stop, **k):
                return nc.tensor.matmul(o, lhsT, rhs, start=start, stop=stop, **k)

            pe.wait_ge(weights_loaded, 16 * 12)
            pe.wait_ge(eye_ready, 4)
            for d in range(KT):
                for k in range(KT):
                    m = mm(bank[0][0][:, d, 0:EC], w2t_s[:, k, d * P:(d + 1) * P], ablk_s[:, k, :], k == 0, k == KT - 1)
            m.then_inc(wa_psum, 1)
            pe.wait_ge(wa_ready, 1)
            pe.wait_ge(zeros_set, 6 * SLOTS)

            with pe.Fori(1, rounds + 1) as i:
                for s, what, *arg in STEPS:
                    b = bank[s]
                    if what == "prepare":
                        pe.wait_ge(sem("adjf_ready", s), nth("adjf_ready", i, 1))
                        pe.wait_ge(sem("out_ready", s), past("out_ready", i))
                        for k in range(NT):
                            for t in range(NT):
                                m = nc.tensor.transpose(b[0][:, k, t * P:(t + 1) * P], adjf[s][:, t, k * P:(k + 1) * P],
                                                        ident[:])
                        m.then_inc(sem("adjT_psum", s), 1)
                    if what == "norm" and arg[0] in TRANSPOSED:
                        pe.wait_ge(sem("ln_z", s), nth("ln_z", i, 2 * arg[0] + 2))
                        for k in range(KT):
                            for t in range(NT):
                                m = nc.tensor.transpose(b[2][:, k, t * P:(t + 1) * P], z[s][:, t, k * P:(k + 1) * P],
                                                        ident[:])
                        m.then_inc(sem("zT_psum", s), 1)
                    if what == "qkv":
                        layer = arg[0]
                        w = wqkv0_s if layer == 0 else wqkv3_s
                        pe.wait_ge(sem("hT_ready", s), nth("hT_ready", i, HT_DONE[PRE0 if layer == 0 else PRE3]))
                        if layer == 0:
                            pe.wait_ge(sem("adjT_ready", s), nth("adjT_ready", i, 1))
                        else:
                            pe.wait_ge(sem("o2_ready", s), nth("o2_ready", i, 1))
                        for part, name in enumerate(("q_psum", "k_psum")):
                            for g in range(2):
                                c = part * D + g * P
                                for k in range(KT):
                                    m = mm(b[part][:, g, :], w[:, k, c:c + P], hT[s][:, k, :], k == 0, k == KT - 1)
                            m.then_inc(sem(name, s), 1)
                        for t in range(NT):
                            for k in range(KT):
                                m = mm(b[3][:, t, :], hT[s][:, k, t * P:(t + 1) * P], w[:, k, 2 * D:3 * D],
                                       k == 0, k == KT - 1)
                        m.then_inc(sem("v_psum", s), 1)
                    if what == "scores":
                        layer, h = arg
                        a = ATTN[layer][0] + h
                        if layer == 2:
                            pe.wait_ge(sem("uw", s), nth("uw", i, 4 * TYPES * (h + 1)))
                            if h >= 2:
                                pe.wait_ge(sem("z_sum", s), nth("z_sum", i, h - 1))
                            for t in range(NT):
                                for j in range(NT):
                                    m = nc.tensor.transpose(b[a % 2][:, t, j * P:(j + 1) * P],
                                                            ww[s][:, h % 2, j, t * P:(t + 1) * P], ident[:])
                        else:
                            qk = 2 if layer == 0 else 3
                            pe.wait_ge(sem("q_ready", s), nth("q_ready", i, qk))
                            pe.wait_ge(sem("k_ready", s), nth("k_ready", i, qk))
                            if h == 0:
                                if layer == 0:
                                    pe.wait_ge(sem("mask0_ready", s), nth("mask0_ready", i, 1))
                                else:
                                    pe.wait_ge(sem("mask3_ready", s), nth("mask3_ready", i, 1))
                            if h >= 2:
                                pe.wait_ge(sem("probs", s), nth("probs", i, 2 * (a - 1)))
                            g, r = h // 4, HD * (h % 4)
                            mask = mask0[s] if layer == 0 else mask3[s]
                            for t in range(NT):
                                mm(b[a % 2][:, t, :], identb[:], mask[:, t, :], True, False)
                                m = mm(b[a % 2][:, t, :], qT[s][r:r + HD, g, t * P:(t + 1) * P], kT[s][r:r + HD, g, :],
                                       False, True)
                        m.then_inc(sem("s_psum", s), 1)
                    if what == "turn":
                        layer, h = arg
                        a = ATTN[layer][0] + h
                        pe.wait_ge(sem("probs", s), nth("probs", i, 2 * (a + 1)))
                        if a:
                            pe.wait_ge(sem("pT_ready", s), nth("pT_ready", i, a))
                        for j in range(NT):
                            for t in range(NT):
                                m = nc.tensor.transpose(b[2][:, j, t * P:(t + 1) * P],
                                                        pr[s][:, a % 2, t, j * P:(j + 1) * P], ident[:])
                        m.then_inc(sem("pT_psum", s), 1)
                    if what == "weigh":
                        layer, h = arg
                        a = ATTN[layer][0] + h
                        per = 2 if layer == 2 else 4
                        pe.wait_ge(sem("pT_ready", s), nth("pT_ready", i, a + 1))
                        if h == 0:
                            if layer == 2:
                                pe.wait_ge(sem("h2_ready", s), nth("h2_ready", i, 2))
                            else:
                                pe.wait_ge(sem("v_ready", s), nth("v_ready", i, 2 + 2 * (layer == 3)))
                        for j in range(NT):
                            m = mm(b[3][:, h // per, :], head_window(s, layer, h, j), pT[s][:, a % 2, j, :],
                                   h % per == 0 and j == 0, h % per == per - 1 and j == NT - 1)
                        m.then_inc(sem("pv_done", s), 1)
                    if what == "normal":
                        n = ATTN_NO[arg[0]]
                        pe.wait_ge(sem("rwide", s), nth("rwide", i, n + 1))
                        first, heads = ATTN[arg[0]]
                        pe.wait_ge(sem("pT_ready", s), nth("pT_ready", i, first + heads))
                        for k in range(KT):
                            for t in range(NT):
                                m = nc.tensor.transpose(b[2][:, k, t * P:(t + 1) * P],
                                                        rwide[s][:, t, k * P:(k + 1) * P], ident[:])
                        m.then_inc(sem("rT_psum", s), 1)
                    if what == "attn_out":
                        w = wo0_s if arg[0] == 0 else wo3_s
                        pe.wait_ge(sem("ctxT_ready", s), nth("ctxT_ready", i, 1 if arg[0] == 0 else 3))
                        for t in range(NT):
                            for k in range(KT):
                                m = mm(b[0][:, t, :], ctxT[s][:, k, t * P:(t + 1) * P], w[:, k, :], k == 0, k == KT - 1)
                        m.then_inc(sem("wo_psum", s), 1)
                    if what == "ff":
                        pe.wait_ge(sem("hT_ready", s), nth("hT_ready", i, HT_DONE[POST1]))
                        for f in range(4):
                            if f == 2:
                                pe.wait_ge(sem("ff_act", s), nth("ff_act", i, 2))
                            if f == 3:
                                pe.wait_ge(sem("ff_dve", s), nth("ff_dve", i, 2))
                            for u in range(2):
                                c = (2 * f + u) * P
                                for k in range(KT):
                                    m = mm(b[f % 2][:, u, :], w1_s[:, k, c:c + P], hT[s][:, k, :], k == 0, k == KT - 1)
                            m.then_inc(sem("ff1_psum", s), 1)
                        pe.wait_ge(sem("ff_act", s), nth("ff_act", i, 4))
                        pe.wait_ge(sem("ff_dve", s), nth("ff_dve", i, 4))
                        for t in range(NT):
                            for f in range(FT):
                                m = mm(b[3][:, t, :], ffT[s][:, f, t * P:(t + 1) * P], w2_s[:, f, :], f == 0, f == FT - 1)
                        m.then_inc(sem("ff2_psum", s), 1)
                    if what == "mean_step":
                        pe.wait_ge(sem("hT_ready", s), nth("hT_ready", i, HT_DONE[PRE1]))
                        for t in range(NT):
                            for k in range(KT):
                                m = mm(b[t][:].rearrange("p a c -> p (a c)"), hT[s][:, k, t * P:(t + 1) * P],
                                       wl1_s[:, k, :], k == 0, k == KT - 1)
                            m.then_inc(sem("l1_psum", s), 1)
                        pe.wait_ge(sem("hm_ready", s), nth("hm_ready", i, 2))
                        for j in range(NT):
                            o = b[2 + j][:].rearrange("p a c -> p (a c)")[:, 0:D + 1]
                            for t in range(NT):
                                m = mm(o, adjf[s][:, t, j * P:(j + 1) * P], hm[s][:, t, :], t == 0, t == NT - 1)
                            m.then_inc(sem("msg_psum", s), 1)
                    if what == "types_in":
                        pe.wait_ge(sem("hT_ready", s), nth("hT_ready", i, HT_DONE[PRE2]))
                        for t in range(NT):
                            for k in range(KT):
                                m = mm(b[t][:].rearrange("p a c -> p (a c)")[:, 0:D + EC],
                                       hT[s][:, k, t * P:(t + 1) * P], wl2_s[:, k, :], k == 0, k == KT - 1)
                            m.then_inc(sem("l2_psum", s), 1)
                    if what == "types_out":
                        pe.wait_ge(sem("c2_ready", s), nth("c2_ready", i, 2))
                        for t in range(NT):
                            for k in range(KT):
                                m = nc.tensor.transpose(b[0][:, t, k * P:(k + 1) * P], rT[s][:, k, t * P:(t + 1) * P],
                                                        ident[:])
                        m.then_inc(sem("c2_psum", s), 1)

        @block.vector
        def _(dve):
            V = nc.vector
            for s in range(SLOTS):
                for t in range(NT):
                    V.memset(vp[s][:, t, :], 0.0).then_inc(zeros_set, 1)
                    V.memset(vp2[s][:, t, :], 0.0).then_inc(zeros_set, 1)
                    V.memset(hm[s][:, t, D:D + 1], 1.0).then_inc(zeros_set, 1)
            dve.wait_ge(zeros_set, 6 * SLOTS)
            dve.wait_ge(weights_loaded, 16 * 12)
            dve.wait_ge(eye_ready, 5)

            with dve.Fori(1, rounds + 1) as i:
                for s, what, *arg in STEPS:
                    b = bank[s]
                    if what == "norm":
                        ln = arg[0]
                        name, k, src = ln_src[ln]
                        dve.wait_ge(sem(name, s), nth(name, i, k))
                        for t in range(NT):
                            V.bn_stats(st[s][:, t, :], src[s][:, t, :]).then_inc(sem("ln_stats", s), 1)
                        dve.wait_ge(sem("ln_stats", s), nth("ln_stats", i, 2 * ln + 2))
                        dve.sem_inc(wait_carried, 1)
                        for t in range(NT):
                            V.bn_aggr(mv[s][:, t, :], st[s][:, t, :]).then_inc(sem("ln_aggr", s), 1)
                        dve.wait_ge(sem("ln_rstd", s), nth("ln_rstd", i, ln + 1))
                        if ln == PRE1:
                            dve.wait_ge(sem("xa_step", s), nth("xa_step", i, 1))
                        for t in range(NT):
                            V.tensor_scalar(z[s][:, t, :], src[s][:, t, :], mv[s][:, t, 0:1], rstd[s][:, t:t + 1],
                                            ALU.subtract, ALU.mult).then_inc(sem("ln_z", s), 1)
                    if what == "masks":
                        dve.wait_ge(sem("adjT_psum", s), nth("adjT_psum", i, 1))
                        dve.wait_ge(sem("uw", s), past("uw", i))
                        dve.wait_ge(sem("mask2_ready", s), past("mask2_ready", i))
                        dve.wait_ge(sem("types_ready", s), past("types_ready", i))
                        V.tensor_copy(adjT[s][:], b[0][:]).then_inc(sem("adjT_ready", s), 1)
                        dve.wait_ge(sem("adjT_ready", s), nth("adjT_ready", i, 1))
                        V.tensor_tensor(mtmp[s][:], adjf[s][:], adjT[s][:], ALU.max).then_inc(sem("mask0_step", s), 1)
                        dve.wait_ge(sem("mask0_step", s), nth("mask0_step", i, 1))
                        V.tensor_tensor(mtmp[s][:], mtmp[s][:], eye[:], ALU.max).then_inc(sem("mask0_step", s), 1)
                        dve.wait_ge(sem("mask0_step", s), nth("mask0_step", i, 2))
                        V.tensor_scalar(mask0[s][:], mtmp[s][:], 0.0, MASKED, ALU.is_le, ALU.mult)\
                            .then_inc(sem("mask0_ready", s), 1)
                    if what == "qkv":
                        layer = arg[0]
                        dve.wait_ge(sem("q_psum", s), nth("q_psum", i, 1 + (layer == 3)))
                        if layer == 0:
                            for k in range(2):
                                V.tensor_scalar(qT[s][:, k, :], b[0][:, k, :], col("bq", k), QSCALE, ALU.add, ALU.mult)\
                                    .then_inc(sem("q_ready", s), 1)
                            dve.wait_ge(sem("v_psum", s), nth("v_psum", i, 1))
                            for t in range(NT):
                                V.tensor_tensor(vp[s][:, t, 96:VW].rearrange("p (h c) -> p h c", c=P)[:, :, 0:HD],
                                                b[3][:, t, :].rearrange("p (h d) -> p h d", d=HD),
                                                row("bv").rearrange("p (h d) -> p h d", d=HD), ALU.add)\
                                    .then_inc(sem("v_ready", s), 1)
                        else:
                            V.tensor_scalar(qT[s][:], b[0][:], QSCALE, None, ALU.mult).then_inc(sem("q_ready", s), 1)
                    if what == "scores":
                        layer, h = arg
                        a = ATTN[layer][0] + h
                        src = b[a % 2]
                        if layer == 2:
                            if h == 0:
                                dve.wait_ge(sem("types_ready", s), nth("types_ready", i, 2 * TYPES))
                                dve.wait_ge(sem("e_ready", s), nth("e_ready", i, 2))
                            for t in range(TYPES):
                                if t:
                                    dve.wait_ge(sem("uw", s), nth("uw", i, 4 * (TYPES * h + t)))
                                for n in range(NT):
                                    e = esd[s][:, n, H2 * TYPES + h * TYPES + t:H2 * TYPES + h * TYPES + t + 1]
                                    V.scalar_tensor_tensor(ww[s][:, h % 2, n, :], typT[s][:, t, n, :], e,
                                                           ww[s][:, h % 2, n, :] if t else mask2[s][:, n, :],
                                                           ALU.mult, ALU.add).then_inc(sem("uw", s), 1)
                                for n in range(NT):
                                    e = esd[s][:, n, h * TYPES + t:h * TYPES + t + 1]
                                    if t == 0:
                                        V.tensor_scalar(uu[s][:, h % 2, n, :], typ[s][:, t, n, :], e, None, ALU.mult)\
                                            .then_inc(sem("uw", s), 1)
                                    else:
                                        V.scalar_tensor_tensor(uu[s][:, h % 2, n, :], typ[s][:, t, n, :], e,
                                                               uu[s][:, h % 2, n, :], ALU.mult, ALU.add)\
                                            .then_inc(sem("uw", s), 1)
                            dve.wait_ge(sem("s_psum", s), nth("s_psum", i, a + 1))
                            dve.wait_ge(sem("uw", s), nth("uw", i, 4 * TYPES * (h + 1)))
                            V.tensor_tensor(zs[s][:], src[:], uu[s][:, h % 2], ALU.add).then_inc(sem("z_sum", s), 1)
                            dve.wait_ge(sem("z_sum", s), nth("z_sum", i, h + 1))
                            V.scalar_tensor_tensor(zl[s][a % 2][:], zs[s][:], 0.01, zs[s][:], ALU.mult, ALU.max)\
                                .then_inc(sem("z_leaky", s), 1)
                            dve.wait_ge(sem("z_leaky", s), nth("z_leaky", i, h + 1))
                            src = zl[s][a % 2][:]
                        else:
                            dve.wait_ge(sem("s_psum", s), nth("s_psum", i, a + 1))
                        V.tensor_reduce(nmax[s][:, a % 2, :], src[:], AX.X, ALU.max, negate=True)\
                            .then_inc(sem("negmax", s), 1)
                    if what == "weigh" and arg[0] != 2:
                        layer, h = arg
                        a = ATTN[layer][0] + h
                        dve.wait_ge(sem("pT_psum", s), nth("pT_psum", i, a + 1))
                        if a >= 2:
                            dve.wait_ge(sem("pv_done", s), nth("pv_done", i, a - 1))
                        V.tensor_copy(pT[s][:, a % 2], b[2][:]).then_inc(sem("pT_ready", s), 1)
                    if what == "normal":
                        layer = arg[0]
                        n = ATTN_NO[layer]
                        first, heads = ATTN[layer]
                        dve.wait_ge(sem("probs", s), nth("probs", i, 2 * (first + heads)))
                        V.reciprocal(rinv[s][:, :, 0:heads], rsum[s][:, :, 0:heads]).then_inc(sem("rinv", s), 1)
                        dve.wait_ge(sem("rinv", s), nth("rinv", i, n + 1))
                        V.tensor_copy(rwide[s][:].rearrange("p t (h d) -> p t h d", h=heads),
                                      rinv[s][:, :, 0:heads, None].broadcast_to([P, NT, heads, D // heads]))\
                            .then_inc(sem("rwide", s), 1)
                        dve.wait_ge(sem("rT_ready", s), nth("rT_ready", i, n + 1))
                        dve.wait_ge(sem("pv_done", s), nth("pv_done", i, first + heads))
                        V.tensor_tensor(ctxT[s][:], b[3][:], rT[s][:], ALU.mult).then_inc(sem("ctxT_ready", s), 1)
                    if what == "attn_out":
                        if arg[0] == 0:
                            dve.wait_ge(sem("wo_psum", s), nth("wo_psum", i, 1))
                            dve.wait_ge(sem("hb_ready", s), nth("hb_ready", i, 2))
                            V.tensor_tensor(r1[s][:], b[0][:], hb[s][:], ALU.add).then_inc(sem("r1_ready", s), 1)
                        else:
                            dve.wait_ge(sem("wo_psum", s), nth("wo_psum", i, 2))
                            dve.wait_ge(sem("xc_bo", s), nth("xc_bo", i, 1))
                            dve.wait_ge(sem("out_stored", s), past("out_stored", i))
                            V.tensor_tensor(xo[s][:], b[0][:], xc[s][:], ALU.add).then_inc(sem("out_ready", s), 1)
                    if what == "ff":
                        for f in range(1, 4, 2):
                            dve.wait_ge(sem("ff1_psum", s), nth("ff1_psum", i, f + 1))
                            for k in range(2):
                                V.tensor_scalar(ffT[s][:, 2 * f + k, :], b[f % 2][:, k, :], col("b1", 2 * f + k), 0.0,
                                                ALU.add, ALU.max).then_inc(sem("ff_dve", s), 1)
                        dve.wait_ge(sem("ff2_psum", s), nth("ff2_psum", i, 1))
                        dve.wait_ge(sem("r1n_ready", s), nth("r1n_ready", i, 2))
                        V.tensor_tensor(r1[s][:], b[3][:], r1n[s][:], ALU.add).then_inc(sem("r2_ready", s), 1)
                    if what == "mean_step":
                        for t in range(NT):
                            dve.wait_ge(sem("l1_psum", s), nth("l1_psum", i, t + 1))
                            dve.wait_ge(sem("hm_ready", s), nth("hm_ready", i, t + 1))
                            V.tensor_tensor(upd[s][:, t, :], b[t][:, 1, :], row("l1_bias"), ALU.add)\
                                .then_inc(sem("upd_ready", s), 1)
                        for j in range(NT):
                            dve.wait_ge(sem("msg_psum", s), nth("msg_psum", i, j + 1))
                            dg = b[2 + j][:, 1, 0:1]
                            V.tensor_scalar(deg[s][:, j, 0:1], dg, 1.0, None, ALU.max).then_inc(sem("deg_step", s), 1)
                            dve.wait_ge(sem("deg_step", s), nth("deg_step", i, 3 * j + 1))
                            V.reciprocal(deg[s][:, j, 1:2], deg[s][:, j, 0:1]).then_inc(sem("deg_step", s), 1)
                            dve.wait_ge(sem("deg_step", s), nth("deg_step", i, 3 * j + 2))
                            V.scalar_tensor_tensor(deg[s][:, j, 2:3], dg, 0.0, deg[s][:, j, 1:2], ALU.is_gt, ALU.mult)\
                                .then_inc(sem("deg_step", s), 1)
                            dve.wait_ge(sem("deg_step", s), nth("deg_step", i, 3 * j + 3))
                            dve.wait_ge(sem("upd_ready", s), nth("upd_ready", i, j + 1))
                            V.scalar_tensor_tensor(upd[s][:, j, :], b[2 + j][:, 0, :], deg[s][:, j, 2:3], upd[s][:, j, :],
                                                   ALU.mult, ALU.add).then_inc(sem("msg_ready", s), 1)
                        dve.wait_ge(sem("msg_ready", s), nth("msg_ready", i, 2))
                        V.scalar_tensor_tensor(xb[s][:], upd[s][:], 0.0, xa[s][:], ALU.max, ALU.add)\
                            .then_inc(sem("xb_ready", s), 1)
                    if what == "types_in":
                        for t in range(NT):
                            dve.wait_ge(sem("h2_ready", s), nth("h2_ready", i, t + 1))
                            V.tensor_copy(esd[s][:, t, :], b[t][:, 1, 0:EC]).then_inc(sem("e_ready", s), 1)
                    if what == "types_out":
                        dve.wait_ge(sem("c2_psum", s), nth("c2_psum", i, 1))
                        V.tensor_tensor(o2[s][:].rearrange("p t (h d) -> p t h d", d=HO),
                                        b[0][:].rearrange("p t (h d) -> p t h d", d=HO),
                                        vp2[s][:, :, 64:VW2].rearrange("p t (h c) -> p t h c", c=P)[:, :, :, 0:HO],
                                        ALU.add).then_inc(sem("o2_ready", s), 1)
                        dve.wait_ge(sem("o2_ready", s), nth("o2_ready", i, 1))
                        oh = o2[s][:].rearrange("p t (h d) -> p (t h) d", d=HO)
                        for u in range(8):
                            V.bn_stats(hst[s][:, u, :], oh[:, u, :]).then_inc(sem("hln_stats", s), 1)
                        dve.wait_ge(sem("hln_stats", s), nth("hln_stats", i, 8))
                        dve.sem_inc(wait_carried, 1)
                        for u in range(8):
                            V.bn_aggr(hmv[s][:, u, :], hst[s][:, u, :]).then_inc(sem("hln_aggr", s), 1)
                        dve.wait_ge(sem("hln_aggr", s), nth("hln_aggr", i, 8))
                        V.tensor_tensor(oh, oh, hmv[s][:, :, 0:1].broadcast_to([P, 8, HO]), ALU.subtract)\
                            .then_inc(sem("o2_step", s), 1)
                        dve.wait_ge(sem("o2_step", s), nth("o2_step", i, 1))
                        dve.wait_ge(sem("hln_rstd", s), nth("hln_rstd", i, 1))
                        V.tensor_tensor(oh, oh, hrs[s][:, :, None].broadcast_to([P, 8, HO]), ALU.mult)\
                            .then_inc(sem("o2_step", s), 1)


def kernel(**inputs):
    import concourse.bacc as bacc
    from concourse.bass_utils import run_bass_kernel_spmd

    a = {n: np.asarray(v) for n, v in inputs.items()}
    d = np.float32

    def spread(v):
        return np.broadcast_to(np.asarray(v).reshape(1, D), (P, D))

    def columns(v):
        return np.asarray(v).reshape(-1, P).T

    rows = np.stack([spread(v) for v in (
        a["L0_gnn_bqkv"][2 * D:], a["L0_gnn_bo"], a["L0_gnn_ln1_g"], a["L0_gnn_ln1_b"], a["L0_gnn_b2"],
        a["L0_gnn_ln2_g"], a["L0_gnn_ln2_b"], a["L1_gnn_bias"], a["L2_gnn_ln_gamma"], a["L2_gnn_ln_beta"],
        a["L3_gnn_bo"])], axis=1)
    cols = np.concatenate([columns(v) for v in (
        a["L0_gnn_bqkv"][:D], a["L0_gnn_bqkv"][D:2 * D], a["L0_gnn_ln1_g"], a["L0_gnn_ln1_b"], a["L0_gnn_b1"],
        a["L2_gnn_bias"])], axis=1)
    ablk = np.zeros((D, 2, H2, TYPES), d)
    for h in range(H2):
        ablk[h * HO:(h + 1) * HO, 0, h] = a["L2_gnn_a_src"][h].T
        ablk[h * HO:(h + 1) * HO, 1, h] = a["L2_gnn_a_dst"][h].T
    arrays = {
        "x": a["x"], "adj": a["adj"],
        "wqkv0": a["L0_gnn_Wqkv"].T, "wo0": a["L0_gnn_Wo"].T, "w1": a["L0_gnn_W1"].T, "w2": a["L0_gnn_W2"].T,
        "wl1": np.concatenate([a["L1_gnn_W_msg"], a["L1_gnn_W_upd"]], axis=1),
        "wl2": a["L2_gnn_W"].transpose(1, 0, 2).reshape(D, D),
        "w2t": a["L2_gnn_W"].transpose(0, 2, 1).reshape(D, D),
        "ablk": ablk.reshape(D, 2 * H2 * TYPES),
        "wqkv3": np.concatenate([a["L3_gnn_Wq"], a["L3_gnn_Wk"], a["L3_gnn_Wv"]], axis=1),
        "wo3": a["L3_gnn_Wo"], "rows": rows, "cols": cols,
    }
    arrays = {n: np.ascontiguousarray(v) for n, v in arrays.items()}
    nc = bacc.Bacc("TRN2", target_bir_lowering=False, num_devices=1)
    args = [nc.dram_tensor(n, v.shape, mybir.dt.from_np(v.dtype), kind="ExternalInput").ap() for n, v in arrays.items()]
    out = nc.dram_tensor("out", a["x"].shape, F32, kind="ExternalOutput").ap()
    build(nc, *args, out)
    r = run_bass_kernel_spmd(nc, [arrays], core_ids=[0])
    return r.results[0]["out"]
```

```python
from contextlib import ExitStack

import numpy as np

import concourse.bass as bass
from concourse import mybir

ALU = mybir.AluOpType
ACT = mybir.ActivationFunctionType
AX = mybir.AxisListType
F32 = mybir.dt.float32
BF16 = mybir.dt.bfloat16
I32 = mybir.dt.int32

P = 128
N = 256
D = 256
NT = N // P
KT = D // P
HEADS, HD = 8, 32
H2, HO = 4, 64
TYPES = 5
FF = 1024
FT = FF // P
SLOTS = 2
MASKED = -float(2 ** 100)
EPS_L0, EPS_PRE, EPS_L2 = 1e-5, 1e-5, 1e-6
QSCALE = float(np.float32(1.0 / np.sqrt(HD)))

ROWS = ["bv", "bo0", "ln1_g", "ln1_b", "b2", "ln2_g", "ln2_b", "l1_bias", "l2_g", "l2_b", "bo3"]
COLS = {"bq": (0, 2), "bk": (2, 2), "ln1_g": (4, 2), "ln1_b": (6, 2), "b1": (8, FT), "l2_bias": (8 + FT, 2)}
NCOLS = 10 + FT

PRE0, POST1, POST2, PRE1, PRE2, PRE3 = range(6)
TRANSPOSED = {PRE0: 0, POST1: 1, PRE1: 2, PRE2: 3, PRE3: 4}
HT_DONE = {PRE0: 1, POST1: 3, PRE1: 4, PRE2: 5, PRE3: 6}
ATTN = {0: (0, HEADS), 2: (HEADS, H2), 3: (HEADS + H2, HEADS)}
ATTN_NO = {0: 0, 2: 1, 3: 2}
ALL_HEADS = 2 * HEADS + H2

PER_GRAPH = {
    "x_loaded": 16, "adj_loaded": 16, "out_stored": 16,
    "adjf_ready": 1, "adjT_psum": 1, "adjT_ready": 1, "mask0_step": 2, "mask0_ready": 1, "mask3_ready": 1,
    "mask2_ready": 1, "one_ready": 2, "beyond_step": 2, "beyond_col": 1, "beyond_psum": 1, "beyond_flag": 1,
    "ln_stats": 2 * 6, "ln_aggr": 2 * 6, "ln_var": 6, "ln_rstd": 6, "ln_z": 2 * 6, "zT_psum": 5, "hT_ready": 6,
    "qk_psum": 4, "v_psum": 2, "q_ready": 3, "k_ready": 3, "v_ready": 4,
    "s_psum": ALL_HEADS, "negmax": ALL_HEADS, "probs": 2 * ALL_HEADS, "pT_psum": ALL_HEADS, "pT_ready": ALL_HEADS,
    "pv_done": ALL_HEADS,
    "rinv": 3, "rwide": 3, "rT_psum": 3, "rT_ready": 3, "ctxT_ready": 3,
    "hb_ready": 2, "wo_psum": 2, "r1_ready": 1, "r1n_ready": 2, "ff1_psum": 4, "ff_act": 4, "ff_dve": 4,
    "ff2_psum": 2, "r2_ready": 1, "xplus": 1, "gain_step": 2, "xa_ready": 1,
    "l1_psum": 2, "hm_ready": 2, "upd_ready": 2, "msg_psum": 2, "deg_step": 6, "msg_ready": 2, "xb_ready": 1,
    "l2_psum": 2, "h2_ready": 2, "e_ready": 2, "uw": 4 * H2, "others": 6 * (TYPES - 1) * H2, "z_sum": H2, "z_leaky": H2,
    "c2_ready": 2, "c2_psum": 1, "o2_ready": 1, "hln_stats": 8, "hln_aggr": 8, "hln_var": 1, "hln_rstd": 1,
    "o2_step": 2, "xc_ready": 1, "x_bias": 2, "out_ready": 1,
}

PRIMED = ["adjf_ready", "xplus", "ln_z", "msg_psum", "adjT_psum", "r1_ready", "r2_ready", "s_psum", "uw", "xa_ready",
          "xb_ready", "x_bias", "probs", "mask2_ready", "one_ready", "others", "beyond_col", "out_stored"]


def build(nc, x, adj, wqkv0, wo0, w1, w2, wl1, wl2, w2t, ablk, wqkv3, wo3, rows, cols, out):
    nc.disable_value_cache = True
    graphs = x.shape[0]
    rounds = graphs // SLOTS
    x_v = x.rearrange("g (t p) f -> g p t f", p=P)
    adj_v = adj.rearrange("g (t p) f -> g p t f", p=P)
    out_v = out.rearrange("g (t p) f -> g p t f", p=P)
    EC = 2 * H2 * TYPES
    OTHERS = 6 * (TYPES - 1)

    with ExitStack() as ctx:
        def sb(name, shape, dt=F32):
            return ctx.enter_context(nc.sbuf_tensor(name, shape, dt))

        def slots(name, shape, dt=F32):
            return [sb(f"{name}{s}", shape, dt) for s in range(SLOTS)]

        wqkv0_s = sb("wqkv0_s", [P, KT, 3 * D])
        wo0_s = sb("wo0_s", [P, KT, D])
        w1_s = sb("w1_s", [P, KT, FF])
        w2_s = sb("w2_s", [P, FT, D])
        wl1_s = sb("wl1_s", [P, KT, 2 * D])
        wl2_s = sb("wl2_s", [P, KT, D + EC])
        ablk_s = sb("ablk_s", [P, KT, EC])
        wqkv3_s = sb("wqkv3_s", [P, KT, 3 * D])
        wo3_s = sb("wo3_s", [P, KT, D])
        rows_s = sb("rows_s", [P, len(ROWS), D])
        cols_s = sb("cols_s", [P, NCOLS])
        lnb2 = sb("lnb2", [P, D])
        ident = sb("ident", [P, P])
        identb = sb("identb", [P, P], BF16)
        eye = sb("eye", [P, NT, N], BF16)
        power = sb("power", [P, 8])
        ones = sb("ones", [P, P])

        xin, adji = slots("xin", [P, NT, D]), slots("adji", [P, NT, N], I32)
        adjf = slots("adjf", [P, NT, N])
        mask0, mask3 = slots("mask0", [P, NT, N], BF16), slots("mask3", [P, NT, N], BF16)
        mask2 = slots("mask2", [P, NT, N], BF16)
        adjT = slots("adjT", [P, NT, N])
        one, oneT = slots("one", [P, NT, N], BF16), slots("oneT", [P, NT, N], BF16)
        other, otherT = sb("other", [P, NT, N], BF16), sb("otherT", [P, NT, N], BF16)
        beyond, beyond_col = slots("beyond", [P, NT, N]), slots("beyond_col", [P, 1])
        beyond_flag = slots("beyond_flag", [P, 1], I32)
        st, mv, var = slots("st", [P, NT, 6]), slots("mv", [P, NT, 2]), slots("var", [P, NT])
        rstd = slots("rstd", [P, NT])
        z, hT = slots("z", [P, NT, D]), slots("hT", [P, KT, N])
        qT, kT = slots("qT", [P, 2, N]), slots("kT", [P, 2, N])
        VW = HEADS * P + 96
        vp = slots("vp", [P, NT, VW])
        VW2 = H2 * P + 64
        vp2 = slots("vp2", [P, NT, VW2])
        nmax = slots("nmax", [P, 2, NT])
        pr, pT = slots("pr", [P, 2, NT, N]), slots("pT", [P, 2, NT, N])
        rsum, rinv = slots("rsum", [P, NT, HEADS]), slots("rinv", [P, NT, HEADS])
        rwide, rT, ctxT = slots("rwide", [P, NT, D]), slots("rT", [P, KT, N]), slots("ctxT", [P, KT, N])
        r1 = slots("r1", [P, NT, D])
        ffT = slots("ffT", [P, FT, N])
        xa, xb, xc = (slots(n, [P, NT, D]) for n in ("xa", "xb", "xc"))
        hm = slots("hm", [P, NT, D + 1])
        deg = slots("deg", [P, NT, 3])
        esd = slots("esd", [P, NT, EC])
        hst, hmv = slots("hst", [P, 8, 6]), slots("hmv", [P, 8, 2])
        hvar, hrs = slots("hvar", [P, 8]), slots("hrs", [P, 8])
        xo = slots("xo", [P, NT, D])

        ww = [m[:, 0:4, :].rearrange("p (a t) n -> p a t n", a=2) for m in ffT]
        uu = [m[:, 4:8, :].rearrange("p (a t) n -> p a t n", a=2) for m in ffT]
        mtmp = zs = rT
        hb = upd = o2 = r1
        r1n = rwide
        zl = [[z[s], rwide[s]] for s in range(SLOTS)]
        xplus = xb
        w2t_s = pT[0][:, 0]

        bank = [[ctx.enter_context(nc.psum_tensor(f"bank{s}{b}", [P, 2, 256], F32)) for b in range(4)]
                for s in range(SLOTS)]

        sems = {n: [ctx.enter_context(nc.semaphore(f"{n}{s}")) for s in range(SLOTS)] for n in PER_GRAPH}
        weights_loaded = ctx.enter_context(nc.semaphore("weights_loaded"))
        consts_set = ctx.enter_context(nc.semaphore("consts_set"))
        zeros_set = ctx.enter_context(nc.semaphore("zeros_set"))
        eye_ready = ctx.enter_context(nc.semaphore("eye_ready"))
        wait_carried = ctx.enter_context(nc.semaphore("wait_carried"))
        wa_psum = ctx.enter_context(nc.semaphore("wa_psum"))
        wa_ready = ctx.enter_context(nc.semaphore("wa_ready"))

        def row(name):
            return rows_s[:, ROWS.index(name), :]

        def rowt(name):
            r = ROWS.index(name)
            return rows_s[:, r:r + 1, :].broadcast_to([P, NT, D])

        def col(name, k):
            c = COLS[name][0] + k
            return cols_s[:, c:c + 1]

        def sem(name, s):
            return sems[name][s]

        def nth(name, i, k):
            return i * PER_GRAPH[name] + (k if name in PRIMED else k - PER_GRAPH[name])

        def past(name, i):
            assert name in PRIMED
            return i * PER_GRAPH[name]

        def head_window(s, layer, h, t):
            if layer == 2:
                a = h * P + 64 - HO * (h % 2)
                return vp2[s][:, t, a:a + P]
            a = h * P + 96 - HD * (h % 4)
            return vp[s][:, t, a:a + P]

        def attention(layer):
            n = ATTN[layer][1]
            if layer == 2:
                yield (1, "edges", layer, 0)
            for k in range(n + 2):
                if layer == 2 and k + 1 < n:
                    yield (0.2, "edges", layer, k + 1)
                if k < n:
                    yield (1.4 + 0.8 * (layer == 2), "scores", layer, k)
                if k == n + 1:
                    yield (0.5, "spread", layer)
                if k >= 2:
                    yield (1, "weigh", layer, k - 2)
                if 1 <= k <= n:
                    yield (0.7, "turn", layer, k - 1)
                    yield (0, "move", layer, k - 1)
                if k == n:
                    yield (0.7, "widen", layer)
            yield (1, "normal", layer)

        FIRST = [(0.5, "prepare"), (4, "stats", PRE0), (1, "norm", PRE0), (1, "masks"), (6, "qkv", 0), *attention(0),
                 (3, "attn_out", 0), (6, "stats", POST1), (1, "norm", POST1), *((1.7, "ff1", f) for f in range(4)),
                 (3.4, "ff2", 0), (3.4, "ff2", 1), (6, "stats", POST2), (1, "add0")]
        SECOND = [(6, "stats", PRE1), (1, "norm", PRE1), (4, "mean_in"), (4, "mean_out"), (6, "stats", PRE2),
                  (1, "norm", PRE2), (3, "types_in"), *attention(2), (3, "types_out"), (8, "types_norm"),
                  (6, "stats", PRE3), (1, "norm", PRE3), (6, "qkv", 3), *attention(3), (3, "attn_out", 3)]

        def beside(one_half, s1, ahead1, other_half, s2, ahead2):
            total1, total2 = sum(p[0] for p in one_half), sum(p[0] for p in other_half)
            at1, at2, both = 0, 0, []
            one_half, other_half = list(one_half), list(other_half)
            while one_half or other_half:
                if other_half and (not one_half or at2 * total1 < at1 * total2):
                    us, *step = other_half.pop(0)
                    at2 += us
                    both.append((s2, ahead2, *step))
                else:
                    us, *step = one_half.pop(0)
                    at1 += us
                    both.append((s1, ahead1, *step))
            return both

        OPENING = [(1, 0, *step) for _, *step in FIRST]
        ROUND = beside(FIRST, 0, 0, SECOND, 1, 0) + beside(SECOND, 0, 0, FIRST, 1, 1)
        CLOSING = beside(FIRST, 0, 0, SECOND, 1, 0) + [(0, 0, *step) for _, *step in SECOND]

        ln_src = {PRE0: ("x_loaded", 16, xin), POST1: ("r1_ready", 1, r1), POST2: ("r2_ready", 1, r1),
                  PRE1: ("xa_ready", 1, xa), PRE2: ("xb_ready", 1, xb), PRE3: ("xc_ready", 1, xc)}

        block = ctx.enter_context(nc.Block())

        @block.sync
        def _(sp):
            for name in PRIMED:
                for s in range(SLOTS):
                    sp.sem_inc(sem(name, s), PER_GRAPH[name])
            for dst, src in ((wqkv0_s, wqkv0), (wo0_s, wo0), (w1_s, w1), (w2_s, w2), (wl1_s, wl1),
                             (w2t_s, w2t), (ablk_s, ablk), (wqkv3_s, wqkv3), (wo3_s, wo3)):
                sp.dma_start(dst[:] if dst is not w2t_s else dst, src.rearrange("(t p) n -> p t n", p=P)).then_inc(weights_loaded, 16)
            sp.dma_start(wl2_s[:, :, 0:D], wl2.rearrange("(t p) n -> p t n", p=P)).then_inc(weights_loaded, 16)
            sp.dma_start(rows_s[:], rows).then_inc(weights_loaded, 16)
            sp.dma_start(cols_s[:], cols).then_inc(weights_loaded, 16)

            def load(s, i):
                sp.wait_ge(sem("adjf_ready", s), past("adjf_ready", i))
                sp.sem_inc(wait_carried, 1)
                sp.dma_start(adji[s][:], adj_v[i * SLOTS + (s - SLOTS)]).then_inc(sem("adj_loaded", s), 16)
                sp.wait_ge(sem("xplus", s), past("xplus", i))
                sp.sem_inc(wait_carried, 1)
                sp.wait_ge(sem("ln_z", s), past("ln_z", i))
                sp.sem_inc(wait_carried, 1)
                sp.dma_start(xin[s][:], x_v[i * SLOTS + (s - SLOTS)]).then_inc(sem("x_loaded", s), 16)

            def store(s, i):
                sp.wait_ge(sem("out_ready", s), nth("out_ready", i, 1))
                sp.sem_inc(wait_carried, 1)
                sp.dma_start(out_v[i * SLOTS + (s - SLOTS)], xo[s][:]).then_inc(sem("out_stored", s), 16)

            load(1, 1)
            load(0, 1)
            with sp.Fori(1, rounds) as i:
                load(1, i + 1)
                store(1, i)
                load(0, i + 1)
                store(0, i)
            store(1, rounds)
            store(0, rounds)
            for s in range(SLOTS):
                sp.wait_ge(sem("out_stored", s), 16 * (rounds + 1))

        @block.gpsimd
        def _(pool):
            nc.gpsimd.memset(power[:], -0.5).then_inc(consts_set, 1)
            nc.gpsimd.memset(ones[:], 1.0).then_inc(consts_set, 1)
            nc.gpsimd.memset(ident[:], 0.0).then_inc(consts_set, 1)
            nc.gpsimd.memset(identb[:], 0.0).then_inc(consts_set, 1)
            nc.gpsimd.memset(eye[:], 0.0).then_inc(consts_set, 1)
            pool.wait_ge(consts_set, 5)
            for m in (ident, identb):
                nc.gpsimd.affine_select(out=m[:], in_=m[:], compare_op=ALU.not_equal, fill=1.0, base=0,
                                        pattern=[[-1, P]], channel_multiplier=1).then_inc(eye_ready, 1)
            for t in range(NT):
                nc.gpsimd.affine_select(out=eye[:, t, :], in_=eye[:, t, :], compare_op=ALU.not_equal, fill=1.0,
                                        base=t * P, pattern=[[-1, N]], channel_multiplier=1).then_inc(eye_ready, 1)
            pool.wait_ge(weights_loaded, 16 * 12)
            nc.gpsimd.tensor_tensor(lnb2[:], row("ln1_b"), row("b2"), ALU.add).then_inc(eye_ready, 1)
            pool.wait_ge(eye_ready, 5)

            def powered(i, s, eps, src, tmp, dst, steps, done, n, k):
                nc.gpsimd.tensor_scalar(tmp, src, eps, None, ALU.add).then_inc(sem(steps, s), 1)
                pool.wait_ge(sem(steps, s), nth(steps, i, k + 1))
                pool.sem_inc(wait_carried, 1)
                nc.gpsimd.tensor_tensor(dst, tmp, power[:, 0:n], ALU.pow).then_inc(sem(done, s), 1)

            def go(steps, graph):
                for s, ahead, what, *arg in steps:
                    i = graph + ahead
                    if what == "prepare":
                        pool.wait_ge(sem("adj_loaded", s), nth("adj_loaded", i, 16))
                        pool.sem_inc(wait_carried, 1)
                        pool.wait_ge(sem("msg_psum", s), past("msg_psum", i))
                        pool.sem_inc(wait_carried, 1)
                        pool.wait_ge(sem("adjT_psum", s), past("adjT_psum", i))
                        pool.sem_inc(wait_carried, 1)
                        nc.gpsimd.tensor_copy(adjf[s][:], adji[s][:]).then_inc(sem("adjf_ready", s), 1)
                    if what == "stats":
                        ln = arg[0]
                        pool.wait_ge(sem("ln_aggr", s), nth("ln_aggr", i, 2 * ln + 2))
                        pool.sem_inc(wait_carried, 1)
                        powered(i, s, EPS_PRE, mv[s][:, :, 1], var[s][:], rstd[s][:], "ln_var", "ln_rstd", NT, ln)
                        if ln == PRE0:
                            pool.wait_ge(sem("ln_z", s), nth("ln_z", i, 2))
                            pool.sem_inc(wait_carried, 1)
                            pool.wait_ge(sem("r1_ready", s), past("r1_ready", i))
                            pool.sem_inc(wait_carried, 1)
                            nc.gpsimd.tensor_scalar(hb[s][:], z[s][:], 0.0, None, ALU.max).then_inc(sem("hb_ready", s), 1)
                            pool.wait_ge(sem("hb_ready", s), nth("hb_ready", i, 1))
                            pool.sem_inc(wait_carried, 1)
                            nc.gpsimd.tensor_tensor(hb[s][:], hb[s][:], rowt("bo0"), ALU.add)\
                                .then_inc(sem("hb_ready", s), 1)
                        if ln == POST1:
                            pool.wait_ge(sem("ln_z", s), nth("ln_z", i, 4))
                            pool.sem_inc(wait_carried, 1)
                            pool.wait_ge(sem("r2_ready", s), past("r2_ready", i))
                            pool.sem_inc(wait_carried, 1)
                            nc.gpsimd.tensor_tensor(r1n[s][:], z[s][:], rowt("ln1_g"), ALU.mult)\
                                .then_inc(sem("r1n_ready", s), 1)
                            pool.wait_ge(sem("r1n_ready", s), nth("r1n_ready", i, 1))
                            pool.sem_inc(wait_carried, 1)
                            nc.gpsimd.tensor_tensor(r1n[s][:], r1n[s][:], lnb2[:, None, :].broadcast_to([P, NT, D]), ALU.add)\
                                .then_inc(sem("r1n_ready", s), 1)
                    if what == "masks":
                        pool.wait_ge(sem("s_psum", s), past("s_psum", i))
                        pool.sem_inc(wait_carried, 1)
                        nc.gpsimd.tensor_scalar(mask3[s][:], adjf[s][:], 0.0, MASKED, ALU.is_le, ALU.mult)\
                            .then_inc(sem("mask3_ready", s), 1)
                        pool.wait_ge(sem("adjT_ready", s), nth("adjT_ready", i, 1))
                        pool.sem_inc(wait_carried, 1)
                        pool.wait_ge(sem("uw", s), past("uw", i))
                        pool.sem_inc(wait_carried, 1)
                        nc.gpsimd.tensor_scalar(mask2[s][:], adjT[s][:], 0.0, MASKED, ALU.is_equal, ALU.mult)\
                            .then_inc(sem("mask2_ready", s), 1)
                        nc.gpsimd.tensor_scalar(one[s][:], adjf[s][:], 1.0, None, ALU.is_equal)\
                            .then_inc(sem("one_ready", s), 1)
                        nc.gpsimd.tensor_scalar(oneT[s][:], adjT[s][:], 1.0, None, ALU.is_equal)\
                            .then_inc(sem("one_ready", s), 1)
                        pool.wait_ge(sem("beyond_col", s), past("beyond_col", i))
                        pool.sem_inc(wait_carried, 1)
                        nc.gpsimd.tensor_scalar(beyond[s][:], adjf[s][:], -1.0, None, ALU.add)\
                            .then_inc(sem("beyond_step", s), 1)
                        pool.wait_ge(sem("beyond_step", s), nth("beyond_step", i, 1))
                        pool.sem_inc(wait_carried, 1)
                        nc.gpsimd.tensor_tensor(beyond[s][:], beyond[s][:], adjf[s][:], ALU.mult)\
                            .then_inc(sem("beyond_step", s), 1)
                        pool.wait_ge(sem("xa_ready", s), past("xa_ready", i))
                        pool.sem_inc(wait_carried, 1)
                        nc.gpsimd.tensor_tensor(xplus[s][:], xin[s][:], rowt("ln2_b"), ALU.add)\
                            .then_inc(sem("xplus", s), 1)
                    if what == "types_in":
                        pool.wait_ge(sem("ln_z", s), nth("ln_z", i, 10))
                        pool.sem_inc(wait_carried, 1)
                        nc.gpsimd.tensor_tensor(xb[s][:], xb[s][:], rowt("l2_b"), ALU.add).then_inc(sem("x_bias", s), 1)
                    if what == "types_norm":
                        pool.wait_ge(sem("hln_aggr", s), nth("hln_aggr", i, 8))
                        pool.sem_inc(wait_carried, 1)
                        powered(i, s, EPS_L2, hmv[s][:, :, 1], hvar[s][:], hrs[s][:], "hln_var", "hln_rstd", 8, 0)
                    if what == "qkv" and arg[0] == 3:
                        pool.wait_ge(sem("ln_z", s), nth("ln_z", i, 12))
                        pool.sem_inc(wait_carried, 1)
                        pool.wait_ge(sem("xc_ready", s), nth("xc_ready", i, 1))
                        pool.sem_inc(wait_carried, 1)
                        nc.gpsimd.tensor_tensor(xc[s][:], xc[s][:], rowt("bo3"), ALU.add).then_inc(sem("x_bias", s), 1)

            go(OPENING, 1)
            with pool.Fori(1, rounds) as i:
                go(ROUND, i)
            go(CLOSING, rounds)

        @block.scalar
        def _(act):
            act.wait_ge(weights_loaded, 16 * 12)
            act.wait_ge(wa_psum, 1)
            nc.scalar.activation(wl2_s[:, :, D:D + EC], bank[0][0][:, :, 0:EC], ACT.Copy).then_inc(wa_ready, 1)
            act.wait_ge(zeros_set, 6 * SLOTS)

            def go(steps, graph):
                for s, ahead, what, *arg in steps:
                    i = graph + ahead
                    b = bank[s]
                    if what == "norm" and arg[0] in TRANSPOSED:
                        ln = arg[0]
                        act.wait_ge(sem("zT_psum", s), nth("zT_psum", i, TRANSPOSED[ln] + 1))
                        if ln == POST1:
                            for k in range(KT):
                                nc.scalar.activation(hT[s][:, k, :], b[2][:, k, :], ACT.Identity,
                                   bias=col("ln1_b", k), scale=col("ln1_g", k)).then_inc(sem("hT_ready", s), 1)
                        else:
                            nc.scalar.activation(hT[s][:], b[2][:], ACT.Relu).then_inc(sem("hT_ready", s), 1)
                    if what == "qkv":
                        act.wait_ge(sem("qk_psum", s), nth("qk_psum", i, 2 + 2 * (arg[0] == 3)))
                        if arg[0] == 0:
                            act.wait_ge(sem("s_psum", s), past("s_psum", i))
                            for k in range(2):
                                nc.scalar.activation(kT[s][:, k, :], b[1][:, k, :], ACT.Identity, bias=col("bk", k)).then_inc(sem("k_ready", s), 1)
                        else:
                            nc.scalar.activation(kT[s][:], b[1][:], ACT.Copy).then_inc(sem("k_ready", s), 1)
                            act.wait_ge(sem("v_psum", s), nth("v_psum", i, 2))
                            for t in range(NT):
                                nc.scalar.activation(vp[s][:, t, 96:VW].rearrange("p (h c) -> p h c", c=P)[:, :, 0:HD],
                                   b[3][:, t, :].rearrange("p (h d) -> p h d", d=HD), ACT.Copy).then_inc(sem("v_ready", s), 1)
                    if what == "turn":
                        layer, h = arg
                        a = ATTN[layer][0] + h
                        act.wait_ge(sem("negmax", s), nth("negmax", i, a + 1))
                        if layer == 2:
                            act.wait_ge(sem("z_leaky", s), nth("z_leaky", i, h + 1))
                        if a >= 2:
                            act.wait_ge(sem("pT_psum", s), nth("pT_psum", i, a - 1))
                        src = zl[s][a % 2][:] if layer == 2 else b[a % 2]
                        for t in range(NT):
                            nc.scalar.activation(pr[s][:, a % 2, t, :], src[:, t, :], ACT.Exp,
                               bias=nmax[s][:, a % 2, t:t + 1], accum_out=rsum[s][:, t, h:h + 1]).then_inc(sem("probs", s), 1)
                    if what == "move" and arg[0] == 2:
                        layer, h = arg
                        a = ATTN[layer][0] + h
                        act.wait_ge(sem("pT_psum", s), nth("pT_psum", i, a + 1))
                        act.wait_ge(sem("pv_done", s), nth("pv_done", i, a - 1))
                        nc.scalar.activation(pT[s][:, a % 2], b[2][:], ACT.Copy).then_inc(sem("pT_ready", s), 1)
                    if what == "spread":
                        n = ATTN_NO[arg[0]]
                        act.wait_ge(sem("rT_psum", s), nth("rT_psum", i, n + 1))
                        nc.scalar.activation(rT[s][:], b[2][:], ACT.Copy).then_inc(sem("rT_ready", s), 1)
                    if what == "ff1" and arg[0] % 2 == 0:
                        f = arg[0]
                        act.wait_ge(sem("ff1_psum", s), nth("ff1_psum", i, f + 1))
                        for k in range(2):
                                nc.scalar.activation(ffT[s][:, 2 * f + k, :], b[f % 2][:, k, :], ACT.Relu,
                                   bias=col("b1", 2 * f + k)).then_inc(sem("ff_act", s), 1)
                    if what == "mean_in":
                        for t in range(NT):
                            act.wait_ge(sem("l1_psum", s), nth("l1_psum", i, t + 1))
                            nc.scalar.activation(hm[s][:, t, 0:D], b[t][:, 0, :], ACT.Copy).then_inc(sem("hm_ready", s), 1)
                    if what == "types_in":
                        for t in range(NT):
                            act.wait_ge(sem("l2_psum", s), nth("l2_psum", i, t + 1))
                            nc.scalar.activation(vp2[s][:, t, 64:VW2].rearrange("p (h c) -> p h c", c=P)[:, :, 0:HO],
                               b[t][:, 0, :].rearrange("p (h d) -> p h d", d=HO), ACT.Copy).then_inc(sem("h2_ready", s), 1)
                    if what == "types_out":
                        act.wait_ge(sem("ctxT_ready", s), nth("ctxT_ready", i, 2))
                        for k in range(KT):
                            nc.scalar.activation(rT[s][:, k, :], ctxT[s][:, k, :], ACT.Relu, bias=col("l2_bias", k)).then_inc(sem("c2_ready", s), 1)

            go(OPENING, 1)
            with act.Fori(1, rounds) as i:
                go(ROUND, i)
            go(CLOSING, rounds)

        @block.tensor
        def _(pe):
            def mm(o, lhsT, rhs, start, stop, **k):
                return nc.tensor.matmul(o, lhsT, rhs, start=start, stop=stop, **k)

            pe.wait_ge(weights_loaded, 16 * 12)
            pe.wait_ge(eye_ready, 4)
            for d in range(KT):
                for k in range(KT):
                    m = mm(bank[0][0][:, d, 0:EC], w2t_s[:, k, d * P:(d + 1) * P], ablk_s[:, k, :], k == 0, k == KT - 1)
            m.then_inc(wa_psum, 1)
            pe.wait_ge(wa_ready, 1)
            pe.wait_ge(zeros_set, 6 * SLOTS)

            def go(steps, graph):
                for s, ahead, what, *arg in steps:
                    i = graph + ahead
                    b = bank[s]
                    if what == "prepare":
                        pe.wait_ge(sem("adjf_ready", s), nth("adjf_ready", i, 1))
                        pe.wait_ge(sem("probs", s), past("probs", i))
                        for k in range(NT):
                            for t in range(NT):
                                m = nc.tensor.transpose(b[1][:, k, t * P:(t + 1) * P], adjf[s][:, t, k * P:(k + 1) * P],
                                                        ident[:])
                        m.then_inc(sem("adjT_psum", s), 1)
                    if what == "norm" and arg[0] in TRANSPOSED:
                        pe.wait_ge(sem("ln_z", s), nth("ln_z", i, 2 * arg[0] + 2))
                        for k in range(KT):
                            for t in range(NT):
                                m = nc.tensor.transpose(b[2][:, k, t * P:(t + 1) * P], z[s][:, t, k * P:(k + 1) * P],
                                                        ident[:])
                        m.then_inc(sem("zT_psum", s), 1)
                    if what == "qkv":
                        layer = arg[0]
                        w = wqkv0_s if layer == 0 else wqkv3_s
                        pe.wait_ge(sem("hT_ready", s), nth("hT_ready", i, HT_DONE[PRE0 if layer == 0 else PRE3]))
                        if layer == 0:
                            pe.wait_ge(sem("adjT_ready", s), nth("adjT_ready", i, 1))
                            pe.wait_ge(sem("ln_z", s), nth("ln_z", i, 2))
                        else:
                            pe.wait_ge(sem("o2_ready", s), nth("o2_ready", i, 1))
                        for part in range(2):
                            for g in range(2):
                                c = part * D + g * P
                                for k in range(KT):
                                    m = mm(b[part][:, g, :], w[:, k, c:c + P], hT[s][:, k, :], k == 0, k == KT - 1)
                            m.then_inc(sem("qk_psum", s), 1)
                        for t in range(NT):
                            for k in range(KT):
                                m = mm(b[3][:, t, :], hT[s][:, k, t * P:(t + 1) * P], w[:, k, 2 * D:3 * D],
                                       k == 0, k == KT - 1)
                        m.then_inc(sem("v_psum", s), 1)
                    if what == "scores":
                        layer, h = arg
                        a = ATTN[layer][0] + h
                        if layer == 2:
                            pe.wait_ge(sem("uw", s), nth("uw", i, 4 * (h + 1)))
                            pe.wait_ge(sem("others", s), nth("others", i, OTHERS * (h + 1)))
                            if h >= 2:
                                pe.wait_ge(sem("z_sum", s), nth("z_sum", i, h - 1))
                            for t in range(NT):
                                for j in range(NT):
                                    m = nc.tensor.transpose(b[a % 2][:, t, j * P:(j + 1) * P],
                                                            ww[s][:, h % 2, j, t * P:(t + 1) * P], ident[:])
                        else:
                            qk = 2 if layer == 0 else 3
                            pe.wait_ge(sem("q_ready", s), nth("q_ready", i, qk))
                            pe.wait_ge(sem("k_ready", s), nth("k_ready", i, qk))
                            if h == 0:
                                if layer == 0:
                                    pe.wait_ge(sem("mask0_ready", s), nth("mask0_ready", i, 1))
                                else:
                                    pe.wait_ge(sem("mask3_ready", s), nth("mask3_ready", i, 1))
                            if h >= 2:
                                pe.wait_ge(sem("probs", s), nth("probs", i, 2 * (a - 1)))
                            g, r = h // 4, HD * (h % 4)
                            mask = mask0[s] if layer == 0 else mask3[s]
                            for t in range(NT):
                                mm(b[a % 2][:, t, :], identb[:], mask[:, t, :], True, False)
                                m = mm(b[a % 2][:, t, :], qT[s][r:r + HD, g, t * P:(t + 1) * P], kT[s][r:r + HD, g, :],
                                       False, True)
                        m.then_inc(sem("s_psum", s), 1)
                    if what == "turn":
                        layer, h = arg
                        a = ATTN[layer][0] + h
                        pe.wait_ge(sem("probs", s), nth("probs", i, 2 * (a + 1)))
                        if a:
                            pe.wait_ge(sem("pT_ready", s), nth("pT_ready", i, a))
                        for j in range(NT):
                            for t in range(NT):
                                m = nc.tensor.transpose(b[2][:, j, t * P:(t + 1) * P],
                                                        pr[s][:, a % 2, t, j * P:(j + 1) * P], ident[:])
                        m.then_inc(sem("pT_psum", s), 1)
                    if what == "weigh":
                        layer, h = arg
                        a = ATTN[layer][0] + h
                        per = 2 if layer == 2 else 4
                        pe.wait_ge(sem("pT_ready", s), nth("pT_ready", i, a + 1))
                        if h == 0:
                            if layer == 2:
                                pe.wait_ge(sem("h2_ready", s), nth("h2_ready", i, 2))
                            else:
                                pe.wait_ge(sem("v_ready", s), nth("v_ready", i, 2 + 2 * (layer == 3)))
                        for j in range(NT):
                            m = mm(b[3][:, h // per, :], head_window(s, layer, h, j), pT[s][:, a % 2, j, :],
                                   h % per == 0 and j == 0, h % per == per - 1 and j == NT - 1)
                        m.then_inc(sem("pv_done", s), 1)
                    if what == "spread":
                        n = ATTN_NO[arg[0]]
                        pe.wait_ge(sem("rwide", s), nth("rwide", i, n + 1))
                        first, heads = ATTN[arg[0]]
                        pe.wait_ge(sem("pT_ready", s), nth("pT_ready", i, first + heads))
                        for k in range(KT):
                            for t in range(NT):
                                m = nc.tensor.transpose(b[2][:, k, t * P:(t + 1) * P],
                                                        rwide[s][:, t, k * P:(k + 1) * P], ident[:])
                        m.then_inc(sem("rT_psum", s), 1)
                    if what == "attn_out":
                        w = wo0_s if arg[0] == 0 else wo3_s
                        pe.wait_ge(sem("ctxT_ready", s), nth("ctxT_ready", i, 1 if arg[0] == 0 else 3))
                        for t in range(NT):
                            for k in range(KT):
                                m = mm(b[0][:, t, :], ctxT[s][:, k, t * P:(t + 1) * P], w[:, k, :], k == 0, k == KT - 1)
                        m.then_inc(sem("wo_psum", s), 1)
                    if what == "ff1":
                        f = arg[0]
                        if f == 0:
                            pe.wait_ge(sem("hT_ready", s), nth("hT_ready", i, HT_DONE[POST1]))
                        if f == 2:
                            pe.wait_ge(sem("ff_act", s), nth("ff_act", i, 2))
                        if f == 3:
                            pe.wait_ge(sem("ff_dve", s), nth("ff_dve", i, 2))
                        for u in range(2):
                            c = (2 * f + u) * P
                            for k in range(KT):
                                m = mm(b[f % 2][:, u, :], w1_s[:, k, c:c + P], hT[s][:, k, :], k == 0, k == KT - 1)
                        m.then_inc(sem("ff1_psum", s), 1)
                    if what == "ff2":
                        t = arg[0]
                        if t == 0:
                            pe.wait_ge(sem("ff_act", s), nth("ff_act", i, 4))
                            pe.wait_ge(sem("ff_dve", s), nth("ff_dve", i, 4))
                        for f in range(FT):
                            m = mm(b[3][:, t, :], ffT[s][:, f, t * P:(t + 1) * P], w2_s[:, f, :], f == 0, f == FT - 1)
                        m.then_inc(sem("ff2_psum", s), 1)
                    if what == "mean_in":
                        pe.wait_ge(sem("hT_ready", s), nth("hT_ready", i, HT_DONE[PRE1]))
                        for t in range(NT):
                            for k in range(KT):
                                m = mm(b[t][:].rearrange("p a c -> p (a c)"), hT[s][:, k, t * P:(t + 1) * P],
                                       wl1_s[:, k, :], k == 0, k == KT - 1)
                            m.then_inc(sem("l1_psum", s), 1)
                    if what == "mean_out":
                        pe.wait_ge(sem("hm_ready", s), nth("hm_ready", i, 2))
                        for j in range(NT):
                            o = b[2 + j][:].rearrange("p a c -> p (a c)")[:, 0:D + 1]
                            for t in range(NT):
                                m = mm(o, adjf[s][:, t, j * P:(j + 1) * P], hm[s][:, t, :], t == 0, t == NT - 1)
                            m.then_inc(sem("msg_psum", s), 1)
                    if what == "types_in":
                        pe.wait_ge(sem("hT_ready", s), nth("hT_ready", i, HT_DONE[PRE2]))
                        pe.wait_ge(sem("beyond_col", s), nth("beyond_col", i, 1))
                        mm(b[1][:, 1, N - 1:N], ones[:], beyond_col[s][:], True, True).then_inc(sem("beyond_psum", s), 1)
                        for t in range(NT):
                            for k in range(KT):
                                m = mm(b[t][:].rearrange("p a c -> p (a c)")[:, 0:D + EC],
                                       hT[s][:, k, t * P:(t + 1) * P], wl2_s[:, k, :], k == 0, k == KT - 1)
                            m.then_inc(sem("l2_psum", s), 1)
                    if what == "types_out":
                        pe.wait_ge(sem("c2_ready", s), nth("c2_ready", i, 2))
                        for t in range(NT):
                            for k in range(KT):
                                m = nc.tensor.transpose(b[0][:, t, k * P:(k + 1) * P], rT[s][:, k, t * P:(t + 1) * P],
                                                        ident[:])
                        m.then_inc(sem("c2_psum", s), 1)

            go(OPENING, 1)
            with pe.Fori(1, rounds) as i:
                go(ROUND, i)
            go(CLOSING, rounds)

        @block.vector
        def _(dve):
            V = nc.vector
            for s in range(SLOTS):
                for t in range(NT):
                    V.memset(vp[s][:, t, :], 0.0).then_inc(zeros_set, 1)
                    V.memset(vp2[s][:, t, :], 0.0).then_inc(zeros_set, 1)
                    V.memset(hm[s][:, t, D:D + 1], 1.0).then_inc(zeros_set, 1)
            dve.wait_ge(zeros_set, 6 * SLOTS)
            dve.wait_ge(weights_loaded, 16 * 12)
            dve.wait_ge(eye_ready, 5)

            def go(steps, graph):
                for s, ahead, what, *arg in steps:
                    i = graph + ahead
                    b = bank[s]
                    if what == "stats":
                        ln = arg[0]
                        name, k, src = ln_src[ln]
                        dve.wait_ge(sem(name, s), nth(name, i, k))
                        for t in range(NT):
                            V.bn_stats(st[s][:, t, :], src[s][:, t, :]).then_inc(sem("ln_stats", s), 1)
                        dve.wait_ge(sem("ln_stats", s), nth("ln_stats", i, 2 * ln + 2))
                        dve.sem_inc(wait_carried, 1)
                        for t in range(NT):
                            V.bn_aggr(mv[s][:, t, :], st[s][:, t, :]).then_inc(sem("ln_aggr", s), 1)
                        dve.wait_ge(sem("ln_rstd", s), nth("ln_rstd", i, ln + 1))
                        for t in range(NT):
                            V.tensor_scalar(z[s][:, t, :], src[s][:, t, :], mv[s][:, t, 0:1], rstd[s][:, t:t + 1],
                                            ALU.subtract, ALU.mult).then_inc(sem("ln_z", s), 1)
                    if what == "masks":
                        dve.wait_ge(sem("adjT_psum", s), nth("adjT_psum", i, 1))
                        dve.wait_ge(sem("uw", s), past("uw", i))
                        dve.wait_ge(sem("mask2_ready", s), past("mask2_ready", i))
                        dve.wait_ge(sem("one_ready", s), past("one_ready", i))
                        V.tensor_copy(adjT[s][:], b[1][:]).then_inc(sem("adjT_ready", s), 1)
                        dve.wait_ge(sem("adjT_ready", s), nth("adjT_ready", i, 1))
                        V.tensor_tensor(mtmp[s][:], adjf[s][:], adjT[s][:], ALU.max).then_inc(sem("mask0_step", s), 1)
                        dve.wait_ge(sem("mask0_step", s), nth("mask0_step", i, 1))
                        V.tensor_tensor(mtmp[s][:], mtmp[s][:], eye[:], ALU.max).then_inc(sem("mask0_step", s), 1)
                        dve.wait_ge(sem("mask0_step", s), nth("mask0_step", i, 2))
                        V.tensor_scalar(mask0[s][:], mtmp[s][:], 0.0, MASKED, ALU.is_le, ALU.mult)\
                            .then_inc(sem("mask0_ready", s), 1)
                        dve.wait_ge(sem("beyond_step", s), nth("beyond_step", i, 2))
                        V.tensor_reduce(beyond_col[s][:], beyond[s][:], AX.XY, ALU.max).then_inc(sem("beyond_col", s), 1)
                    if what == "qkv":
                        layer = arg[0]
                        dve.wait_ge(sem("qk_psum", s), nth("qk_psum", i, 1 + 2 * (layer == 3)))
                        if layer == 0:
                            for k in range(2):
                                V.tensor_scalar(qT[s][:, k, :], b[0][:, k, :], col("bq", k), QSCALE, ALU.add, ALU.mult)\
                                    .then_inc(sem("q_ready", s), 1)
                            dve.wait_ge(sem("v_psum", s), nth("v_psum", i, 1))
                            for t in range(NT):
                                V.tensor_tensor(vp[s][:, t, 96:VW].rearrange("p (h c) -> p h c", c=P)[:, :, 0:HD],
                                                b[3][:, t, :].rearrange("p (h d) -> p h d", d=HD),
                                                row("bv").rearrange("p (h d) -> p h d", d=HD), ALU.add)\
                                    .then_inc(sem("v_ready", s), 1)
                        else:
                            V.tensor_scalar(qT[s][:], b[0][:], QSCALE, None, ALU.mult).then_inc(sem("q_ready", s), 1)
                    if what == "edges":
                        layer, h = arg
                        if h == 0:
                            dve.wait_ge(sem("one_ready", s), nth("one_ready", i, 2))
                            dve.wait_ge(sem("e_ready", s), nth("e_ready", i, 2))
                        src_col, dst_col = h * TYPES, (H2 + h) * TYPES
                        for n in range(NT):
                            V.scalar_tensor_tensor(ww[s][:, h % 2, n, :], oneT[s][:, n, :],
                                                   esd[s][:, n, dst_col:dst_col + 1], mask2[s][:, n, :],
                                                   ALU.mult, ALU.add).then_inc(sem("uw", s), 1)
                            V.tensor_scalar(uu[s][:, h % 2, n, :], one[s][:, n, :],
                                            esd[s][:, n, src_col:src_col + 1], None, ALU.mult)\
                                .then_inc(sem("uw", s), 1)
                        if h == 0:
                            dve.wait_ge(sem("beyond_flag", s), nth("beyond_flag", i, 1))
                            dve.sem_inc(wait_carried, 1)
                        has_others = dve.value_load(beyond_flag[s][0:1, 0:1])
                        with dve.If(has_others):
                            for t in range(1, TYPES):
                                k = OTHERS * h + 6 * (t - 1)
                                dve.wait_ge(sem("others", s), nth("others", i, k))
                                V.tensor_scalar(other[:], adjf[s][:], float(t + 1), None, ALU.is_equal)\
                                    .then_inc(sem("others", s), 1)
                                V.tensor_scalar(otherT[:], adjT[s][:], float(t + 1), None, ALU.is_equal)\
                                    .then_inc(sem("others", s), 1)
                                dve.wait_ge(sem("others", s), nth("others", i, k + 2))
                                dve.wait_ge(sem("uw", s), nth("uw", i, 4 * (h + 1)))
                                for n in range(NT):
                                    V.scalar_tensor_tensor(ww[s][:, h % 2, n, :], otherT[:, n, :],
                                                           esd[s][:, n, dst_col + t:dst_col + t + 1],
                                                           ww[s][:, h % 2, n, :],
                                                           ALU.mult, ALU.add).then_inc(sem("others", s), 1)
                                    V.scalar_tensor_tensor(uu[s][:, h % 2, n, :], other[:, n, :],
                                                           esd[s][:, n, src_col + t:src_col + t + 1],
                                                           uu[s][:, h % 2, n, :],
                                                           ALU.mult, ALU.add).then_inc(sem("others", s), 1)
                        with dve.Else():
                            dve.sem_inc(sem("others", s), OTHERS)
                    if what == "scores":
                        layer, h = arg
                        a = ATTN[layer][0] + h
                        src = b[a % 2]
                        if layer == 2:
                            dve.wait_ge(sem("s_psum", s), nth("s_psum", i, a + 1))
                            dve.wait_ge(sem("uw", s), nth("uw", i, 4 * (h + 1)))
                            V.tensor_tensor(zs[s][:], src[:], uu[s][:, h % 2], ALU.add).then_inc(sem("z_sum", s), 1)
                            dve.wait_ge(sem("z_sum", s), nth("z_sum", i, h + 1))
                            V.scalar_tensor_tensor(zl[s][a % 2][:], zs[s][:], 0.01, zs[s][:], ALU.mult, ALU.max)\
                                .then_inc(sem("z_leaky", s), 1)
                            dve.wait_ge(sem("z_leaky", s), nth("z_leaky", i, h + 1))
                            src = zl[s][a % 2][:]
                        else:
                            dve.wait_ge(sem("s_psum", s), nth("s_psum", i, a + 1))
                        V.tensor_reduce(nmax[s][:, a % 2, :], src[:], AX.X, ALU.max, negate=True)\
                            .then_inc(sem("negmax", s), 1)
                    if what == "move" and arg[0] != 2:
                        layer, h = arg
                        a = ATTN[layer][0] + h
                        dve.wait_ge(sem("pT_psum", s), nth("pT_psum", i, a + 1))
                        if a >= 2:
                            dve.wait_ge(sem("pv_done", s), nth("pv_done", i, a - 1))
                        V.tensor_copy(pT[s][:, a % 2], b[2][:]).then_inc(sem("pT_ready", s), 1)
                    if what == "widen":
                        layer = arg[0]
                        n = ATTN_NO[layer]
                        first, heads = ATTN[layer]
                        dve.wait_ge(sem("probs", s), nth("probs", i, 2 * (first + heads)))
                        V.reciprocal(rinv[s][:, :, 0:heads], rsum[s][:, :, 0:heads]).then_inc(sem("rinv", s), 1)
                        dve.wait_ge(sem("rinv", s), nth("rinv", i, n + 1))
                        V.tensor_copy(rwide[s][:].rearrange("p t (h d) -> p t h d", h=heads),
                                      rinv[s][:, :, 0:heads, None].broadcast_to([P, NT, heads, D // heads]))\
                            .then_inc(sem("rwide", s), 1)
                    if what == "normal":
                        layer = arg[0]
                        n = ATTN_NO[layer]
                        first, heads = ATTN[layer]
                        dve.wait_ge(sem("rT_ready", s), nth("rT_ready", i, n + 1))
                        dve.wait_ge(sem("pv_done", s), nth("pv_done", i, first + heads))
                        V.tensor_tensor(ctxT[s][:], b[3][:], rT[s][:], ALU.mult).then_inc(sem("ctxT_ready", s), 1)
                    if what == "attn_out":
                        if arg[0] == 0:
                            dve.wait_ge(sem("wo_psum", s), nth("wo_psum", i, 1))
                            dve.wait_ge(sem("hb_ready", s), nth("hb_ready", i, 2))
                            V.tensor_tensor(r1[s][:], b[0][:], hb[s][:], ALU.add).then_inc(sem("r1_ready", s), 1)
                        else:
                            dve.wait_ge(sem("wo_psum", s), nth("wo_psum", i, 2))
                            dve.wait_ge(sem("x_bias", s), nth("x_bias", i, 2))
                            dve.wait_ge(sem("out_stored", s), past("out_stored", i))
                            V.tensor_tensor(xo[s][:], b[0][:], xc[s][:], ALU.add).then_inc(sem("out_ready", s), 1)
                    if what == "ff1" and arg[0] % 2 == 1:
                        f = arg[0]
                        dve.wait_ge(sem("ff1_psum", s), nth("ff1_psum", i, f + 1))
                        for k in range(2):
                            V.tensor_scalar(ffT[s][:, 2 * f + k, :], b[f % 2][:, k, :], col("b1", 2 * f + k), 0.0,
                                            ALU.add, ALU.max).then_inc(sem("ff_dve", s), 1)
                    if what == "ff2" and arg[0] == 1:
                        dve.wait_ge(sem("ff2_psum", s), nth("ff2_psum", i, 2))
                        dve.wait_ge(sem("r1n_ready", s), nth("r1n_ready", i, 2))
                        V.tensor_tensor(r1[s][:], b[3][:], r1n[s][:], ALU.add).then_inc(sem("r2_ready", s), 1)
                    if what == "mean_in":
                        for t in range(NT):
                            dve.wait_ge(sem("l1_psum", s), nth("l1_psum", i, t + 1))
                            dve.wait_ge(sem("hm_ready", s), nth("hm_ready", i, t + 1))
                            V.tensor_tensor(upd[s][:, t, :], b[t][:, 1, :], row("l1_bias"), ALU.add)\
                                .then_inc(sem("upd_ready", s), 1)
                    if what == "mean_out":
                        for j in range(NT):
                            dve.wait_ge(sem("msg_psum", s), nth("msg_psum", i, j + 1))
                            dg = b[2 + j][:, 1, 0:1]
                            V.tensor_scalar(deg[s][:, j, 0:1], dg, 1.0, None, ALU.max).then_inc(sem("deg_step", s), 1)
                            dve.wait_ge(sem("deg_step", s), nth("deg_step", i, 3 * j + 1))
                            V.reciprocal(deg[s][:, j, 1:2], deg[s][:, j, 0:1]).then_inc(sem("deg_step", s), 1)
                            dve.wait_ge(sem("deg_step", s), nth("deg_step", i, 3 * j + 2))
                            V.scalar_tensor_tensor(deg[s][:, j, 2:3], dg, 0.0, deg[s][:, j, 1:2], ALU.is_gt, ALU.mult)\
                                .then_inc(sem("deg_step", s), 1)
                            dve.wait_ge(sem("deg_step", s), nth("deg_step", i, 3 * j + 3))
                            dve.wait_ge(sem("upd_ready", s), nth("upd_ready", i, j + 1))
                            V.scalar_tensor_tensor(upd[s][:, j, :], b[2 + j][:, 0, :], deg[s][:, j, 2:3], upd[s][:, j, :],
                                                   ALU.mult, ALU.add).then_inc(sem("msg_ready", s), 1)
                        dve.wait_ge(sem("msg_ready", s), nth("msg_ready", i, 2))
                        V.scalar_tensor_tensor(xb[s][:], upd[s][:], 0.0, xa[s][:], ALU.max, ALU.add)\
                            .then_inc(sem("xb_ready", s), 1)
                    if what == "types_in":
                        for t in range(NT):
                            dve.wait_ge(sem("h2_ready", s), nth("h2_ready", i, t + 1))
                            V.tensor_copy(esd[s][:, t, :], b[t][:, 1, 0:EC]).then_inc(sem("e_ready", s), 1)
                        dve.wait_ge(sem("beyond_psum", s), nth("beyond_psum", i, 1))
                        V.tensor_scalar(beyond_flag[s][:], b[1][:, 1, N - 1:N], 0.0, None, ALU.is_gt)\
                            .then_inc(sem("beyond_flag", s), 1)
                    if what == "types_out":
                        dve.wait_ge(sem("c2_psum", s), nth("c2_psum", i, 1))
                        V.tensor_tensor(o2[s][:].rearrange("p t (h d) -> p t h d", d=HO),
                                        b[0][:].rearrange("p t (h d) -> p t h d", d=HO),
                                        vp2[s][:, :, 64:VW2].rearrange("p t (h c) -> p t h c", c=P)[:, :, :, 0:HO],
                                        ALU.add).then_inc(sem("o2_ready", s), 1)
                    if what == "types_norm":
                        dve.wait_ge(sem("o2_ready", s), nth("o2_ready", i, 1))
                        oh = o2[s][:].rearrange("p t (h d) -> p (t h) d", d=HO)
                        for u in range(8):
                            V.bn_stats(hst[s][:, u, :], oh[:, u, :]).then_inc(sem("hln_stats", s), 1)
                        dve.wait_ge(sem("hln_stats", s), nth("hln_stats", i, 8))
                        dve.sem_inc(wait_carried, 1)
                        for u in range(8):
                            V.bn_aggr(hmv[s][:, u, :], hst[s][:, u, :]).then_inc(sem("hln_aggr", s), 1)
                        dve.wait_ge(sem("hln_aggr", s), nth("hln_aggr", i, 8))
                        V.tensor_tensor(oh, oh, hmv[s][:, :, 0:1].broadcast_to([P, 8, HO]), ALU.subtract)\
                            .then_inc(sem("o2_step", s), 1)
                        dve.wait_ge(sem("o2_step", s), nth("o2_step", i, 1))
                        dve.wait_ge(sem("hln_rstd", s), nth("hln_rstd", i, 1))
                        V.tensor_tensor(oh, oh, hrs[s][:, :, None].broadcast_to([P, 8, HO]), ALU.mult)\
                            .then_inc(sem("o2_step", s), 1)
                        dve.wait_ge(sem("o2_step", s), nth("o2_step", i, 2))
                        dve.wait_ge(sem("x_bias", s), nth("x_bias", i, 1))
                        V.tensor_tensor(o2[s][:], o2[s][:], rowt("l2_g"), ALU.mult).then_inc(sem("gain_step", s), 1)
                        dve.wait_ge(sem("gain_step", s), nth("gain_step", i, 2))
                        V.tensor_tensor(xc[s][:], o2[s][:], xb[s][:], ALU.add).then_inc(sem("xc_ready", s), 1)
                    if what == "add0":
                        dve.wait_ge(sem("ln_z", s), nth("ln_z", i, 6))
                        V.tensor_tensor(r1[s][:], z[s][:], rowt("ln2_g"), ALU.mult).then_inc(sem("gain_step", s), 1)
                        dve.wait_ge(sem("gain_step", s), nth("gain_step", i, 1))
                        dve.wait_ge(sem("xplus", s), nth("xplus", i, 1))
                        V.tensor_tensor(xa[s][:], r1[s][:], xplus[s][:], ALU.add).then_inc(sem("xa_ready", s), 1)

            go(OPENING, 1)
            with dve.Fori(1, rounds) as i:
                go(ROUND, i)
            go(CLOSING, rounds)


def kernel(**inputs):
    import concourse.bacc as bacc
    from concourse.bass_utils import run_bass_kernel_spmd

    a = {n: np.asarray(v) for n, v in inputs.items()}
    d = np.float32

    def spread(v):
        return np.broadcast_to(np.asarray(v).reshape(1, D), (P, D))

    def columns(v):
        return np.asarray(v).reshape(-1, P).T

    rows = np.stack([spread(v) for v in (
        a["L0_gnn_bqkv"][2 * D:], a["L0_gnn_bo"], a["L0_gnn_ln1_g"], a["L0_gnn_ln1_b"], a["L0_gnn_b2"],
        a["L0_gnn_ln2_g"], a["L0_gnn_ln2_b"], a["L1_gnn_bias"], a["L2_gnn_ln_gamma"], a["L2_gnn_ln_beta"],
        a["L3_gnn_bo"])], axis=1)
    cols = np.concatenate([columns(v) for v in (
        a["L0_gnn_bqkv"][:D], a["L0_gnn_bqkv"][D:2 * D], a["L0_gnn_ln1_g"], a["L0_gnn_ln1_b"], a["L0_gnn_b1"],
        a["L2_gnn_bias"])], axis=1)
    ablk = np.zeros((D, 2, H2, TYPES), d)
    for h in range(H2):
        ablk[h * HO:(h + 1) * HO, 0, h] = a["L2_gnn_a_src"][h].T
        ablk[h * HO:(h + 1) * HO, 1, h] = a["L2_gnn_a_dst"][h].T
    arrays = {
        "x": a["x"], "adj": a["adj"],
        "wqkv0": a["L0_gnn_Wqkv"].T, "wo0": a["L0_gnn_Wo"].T, "w1": a["L0_gnn_W1"].T, "w2": a["L0_gnn_W2"].T,
        "wl1": np.concatenate([a["L1_gnn_W_msg"], a["L1_gnn_W_upd"]], axis=1),
        "wl2": a["L2_gnn_W"].transpose(1, 0, 2).reshape(D, D),
        "w2t": a["L2_gnn_W"].transpose(0, 2, 1).reshape(D, D),
        "ablk": ablk.reshape(D, 2 * H2 * TYPES),
        "wqkv3": np.concatenate([a["L3_gnn_Wq"], a["L3_gnn_Wk"], a["L3_gnn_Wv"]], axis=1),
        "wo3": a["L3_gnn_Wo"], "rows": rows, "cols": cols,
    }
    arrays = {n: np.ascontiguousarray(v) for n, v in arrays.items()}
    nc = bacc.Bacc("TRN2", target_bir_lowering=False, num_devices=1)
    args = [nc.dram_tensor(n, v.shape, mybir.dt.from_np(v.dtype), kind="ExternalInput").ap() for n, v in arrays.items()]
    out = nc.dram_tensor("out", a["x"].shape, F32, kind="ExternalOutput").ap()
    build(nc, *args, out)
    r = run_bass_kernel_spmd(nc, [arrays], core_ids=[0])
    return r.results[0]["out"]
```

```python
from contextlib import ExitStack

import numpy as np

import concourse.bass as bass
from concourse import mybir

ALU = mybir.AluOpType
ACT = mybir.ActivationFunctionType
AX = mybir.AxisListType
F32 = mybir.dt.float32
BF16 = mybir.dt.bfloat16
I32 = mybir.dt.int32

P = 128
N = 256
D = 256
NT = N // P
KT = D // P
HEADS, HD = 8, 32
H2, HO = 4, 64
TYPES = 5
FF = 1024
FT = FF // P
SLOTS = 2
MASKED = -float(2 ** 100)
EPS_L0, EPS_PRE, EPS_L2 = 1e-5, 1e-5, 1e-6
QSCALE = float(np.float32(1.0 / np.sqrt(HD)))

ROWS = ["bv", "bo0", "ln1_g", "ln1_b", "b2", "ln2_g", "ln2_b", "l1_bias", "l2_g", "l2_b", "bo3"]
COLS = {"bq": (0, 2), "bk": (2, 2), "ln1_g": (4, 2), "ln1_b": (6, 2), "b1": (8, FT), "l2_bias": (8 + FT, 2)}
NCOLS = 10 + FT

PRE0, POST1, POST2, PRE1, PRE2, PRE3 = range(6)
TRANSPOSED = {PRE0: 0, POST1: 1, PRE1: 2, PRE2: 3, PRE3: 4}
HT_DONE = {PRE0: 1, POST1: 3, PRE1: 4, PRE2: 5, PRE3: 6}
ATTN = {0: (0, HEADS), 2: (HEADS, H2), 3: (HEADS + H2, HEADS)}
ATTN_NO = {0: 0, 2: 1, 3: 2}
ALL_HEADS = 2 * HEADS + H2

AHEAD_OF_NEXT = 4

ATTN_ORDER = {
    0: ("exp", "scores", "top", "turn", "move", "weigh"),
    2: ("scores", "top", "weigh", "exp", "turn", "move"),
    3: ("exp", "scores", "top", "turn", "move", "weigh"),
}
HEADS_BEHIND = {"scores": 0, "top": 0, "exp": 1, "turn": 1, "move": 1, "weigh": 2}

LENGTH = {
    ("next", "stats"): 0.15, ("next", "scale"): 0.5, ("adj_turn",): 0.5, ("stats", POST1): 2, ("stats", POST2): 2,
    ("stats", PRE1): 2, ("stats", PRE2): 2, ("stats", PRE3): 1.92, ("scale", POST1): 3, ("scale", POST2): 3,
    ("scale", PRE1): 3, ("scale", PRE2): 3, ("scale", PRE3): 3.76, ("masks",): 0.9, ("ff1", 0): 1.73,
    ("ff1", 1): 1.36, ("ff1", 2): 1.22, ("ff1", 3): 1.7, ("ff2", 0): 3.4, ("ff2", 1): 3.4, ("mean_in",): 4,
    ("types_in",): 3, ("types_mean",): 3, ("types_center",): 2.5, ("edges", 2): 0.15, ("weigh", 0): 0.8,
    ("weigh", 2): 1, ("weigh", 3): 1, ("widen", 0): 0.7, ("widen", 2): 0.21, ("widen", 3): 1.09, ("spread", 0): 0.4,
    ("spread", 2): 0.5, ("spread", 3): 0.5, ("normal", 0): 0.8, ("normal", 2): 1.9, ("normal", 3): 1.6,
    ("qk", 0): 6.25, ("v", 0): 1.22, ("attn_out", 0): 1.8, ("attn_add", 0): 1.2, ("qk", 3): 3.96, ("v", 3): 2.43,
    ("attn_out", 3): 1.8, ("attn_add", 3): 1.2, ("scores", 0): 1.4, ("top", 0): 0, ("exp", 0): 0, ("turn", 0): 0.7,
    ("move", 0): 0.24, ("scores", 2): 2.2, ("top", 2): 0.75, ("exp", 2): 0, ("turn", 2): 0.88, ("move", 2): 0,
    ("scores", 3): 1.4, ("top", 3): 0, ("exp", 3): 0, ("turn", 3): 0.7, ("move", 3): 0, ("norm", PRE0): 0.5,
    ("relu", PRE0): 0.5, ("norm", POST1): 0.62, ("relu", POST1): 0.5, ("norm", PRE1): 0.5, ("relu", PRE1): 0.5,
    ("norm", PRE2): 0.68, ("relu", PRE2): 0.15, ("norm", PRE3): 0.5, ("relu", PRE3): 0.5, ("gain0",): 0.17,
    ("add0",): 0.5, ("mean_out",): 7.3, ("mean_add",): 1.08, ("types_out",): 1.4, ("types_add",): 0.6,
    ("types_scale",): 0.45, ("types_gain",): 0.37, ("types_end",): 1.65, ("ff_add",): 0.3,
}

PER_GRAPH = {
    "x_loaded": 16, "adj_loaded": 16, "out_stored": 16,
    "adjf_ready": 1, "adjT_psum": 1, "adjT_ready": 1, "mask0_step": 1, "mask0_ready": 1, "mask3_ready": 1,
    "mask2_ready": 1, "one_ready": 2, "beyond_step": 2, "beyond_col": 1, "beyond_psum": 1, "beyond_flag": 1,
    "ln_stats": 2 * 6, "ln_aggr": 2 * 6, "ln_var": 6, "ln_rstd": 6, "ln_z": 2 * 6, "zT_psum": 5, "hT_ready": 6,
    "qk_psum": 4, "v_psum": 2, "q_ready": 3, "k_ready": 3, "v_ready": 4,
    "s_psum": ALL_HEADS, "negmax": ALL_HEADS, "probs": 2 * ALL_HEADS, "pT_psum": ALL_HEADS, "pT_ready": ALL_HEADS,
    "pv_done": ALL_HEADS,
    "rinv": 3, "rwide": 3, "rT_psum": 3, "rT_ready": 3, "ctxT_ready": 6,
    "hb_ready": 2, "wo_psum": 2, "r1_ready": 1, "r1n_ready": 2, "ff1_psum": 4, "ff_act": 4, "ff_dve": 4,
    "ff2_psum": 2, "r2_ready": 1, "xplus": 1, "gain_step": 2, "xa_ready": 1,
    "l1_psum": 2, "hm_ready": 2, "upd_ready": 2, "msg_psum": 2, "deg_step": 6, "msg_ready": 2, "xb_ready": 1,
    "l2_psum": 2, "h2_ready": 2, "e_ready": 2, "uw": 4 * H2, "others": 6 * (TYPES - 1) * H2, "z_sum": H2, "z_leaky": H2,
    "c2_ready": 2, "c2_psum": 1, "o2_ready": 1, "hln_stats": 8, "hln_aggr": 8, "hln_var": 1, "hln_rstd": 1,
    "o2_step": 2, "xc_ready": 1, "x_bias": 2, "out_ready": 1,
}

PRIMED = ["adjf_ready", "xplus", "ln_z", "msg_psum", "adjT_psum", "r1_ready", "r2_ready", "s_psum", "uw", "xa_ready",
          "xb_ready", "x_bias", "probs", "mask2_ready", "one_ready", "others", "beyond_col", "beyond_step", "out_stored", "out_ready"]


def build(nc, x, adj, wqkv0, wo0, w1, w2, wl1, wl2, w2t, ablk, wqkv3, wo3, rows, cols, out):
    nc.disable_value_cache = True
    graphs = x.shape[0]
    rounds = graphs // SLOTS
    x_v = x.rearrange("g (t p) f -> g p t f", p=P)
    adj_v = adj.rearrange("g (t p) f -> g p t f", p=P)
    out_v = out.rearrange("g (t p) f -> g p t f", p=P)
    EC = 2 * H2 * TYPES
    OTHERS = 6 * (TYPES - 1)

    with ExitStack() as ctx:
        def sb(name, shape, dt=F32):
            return ctx.enter_context(nc.sbuf_tensor(name, shape, dt))

        def slots(name, shape, dt=F32):
            return [sb(f"{name}{s}", shape, dt) for s in range(SLOTS)]

        wqkv0_s = sb("wqkv0_s", [P, KT, 3 * D])
        wo0_s = sb("wo0_s", [P, KT, D])
        w1_s = sb("w1_s", [P, KT, FF])
        w2_s = sb("w2_s", [P, FT, D])
        wl1_s = sb("wl1_s", [P, KT, 2 * D])
        wl2_s = sb("wl2_s", [P, KT, D + EC])
        ablk_s = sb("ablk_s", [P, KT, EC])
        wqkv3_s = sb("wqkv3_s", [P, KT, 3 * D])
        wo3_s = sb("wo3_s", [P, KT, D])
        rows_s = sb("rows_s", [P, len(ROWS), D])
        cols_s = sb("cols_s", [P, NCOLS])
        lnb2 = sb("lnb2", [P, D])
        ident = sb("ident", [P, P])
        identb = sb("identb", [P, P], BF16)
        off_diagonal = sb("off_diagonal", [P, NT, N], BF16)
        power = sb("power", [P, 8])
        ones = sb("ones", [P, P])

        xin, adji = slots("xin", [P, NT, D]), slots("adji", [P, NT, N], I32)
        adjf = slots("adjf", [P, NT, N])
        mask0, mask3 = slots("mask0", [P, NT, N], BF16), slots("mask3", [P, NT, N], BF16)
        mask2 = slots("mask2", [P, NT, N], BF16)
        adjT = slots("adjT", [P, NT, N])
        one, oneT = slots("one", [P, NT, N], BF16), slots("oneT", [P, NT, N], BF16)
        other, otherT = sb("other", [P, NT, N], BF16), sb("otherT", [P, NT, N], BF16)
        beyond, beyond_col = slots("beyond", [P, NT, N]), slots("beyond_col", [P, 1])
        beyond_flag = slots("beyond_flag", [P, 1], I32)
        st, mv, var = slots("st", [P, NT, 6]), slots("mv", [P, NT, 2]), slots("var", [P, NT])
        rstd = slots("rstd", [P, NT])
        z, hT = slots("z", [P, NT, D]), slots("hT", [P, KT, N])
        qT, kT = slots("qT", [P, 2, N]), slots("kT", [P, 2, N])
        VW = HEADS * P + 96
        vp = slots("vp", [P, NT, VW])
        VW2 = H2 * P + 64
        vp2 = slots("vp2", [P, NT, VW2])
        nmax = slots("nmax", [P, 2, NT])
        pr, pT = slots("pr", [P, 2, NT, N]), slots("pT", [P, 2, NT, N])
        rsum, rinv = slots("rsum", [P, NT, HEADS]), slots("rinv", [P, NT, HEADS])
        rwide, rT, ctxT = slots("rwide", [P, NT, D]), slots("rT", [P, KT, N]), slots("ctxT", [P, KT, N])
        r1 = slots("r1", [P, NT, D])
        ffT = slots("ffT", [P, FT, N])
        xa, xb, xc = (slots(n, [P, NT, D]) for n in ("xa", "xb", "xc"))
        hm = slots("hm", [P, NT, D + 1])
        deg = slots("deg", [P, NT, 3])
        esd = slots("esd", [P, NT, EC])
        hst, hmv = slots("hst", [P, 8, 6]), slots("hmv", [P, 8, 2])
        hvar, hrs = slots("hvar", [P, 8]), slots("hrs", [P, 8])
        xo = slots("xo", [P, NT, D])

        ww = [m[:, 0:4, :].rearrange("p (a t) n -> p a t n", a=2) for m in ffT]
        uu = [m[:, 4:8, :].rearrange("p (a t) n -> p a t n", a=2) for m in ffT]
        mtmp = zs = rT
        hb = upd = o2 = r1
        r1n = rwide
        zl = [[z[s], rwide[s]] for s in range(SLOTS)]
        xplus = xb
        w2t_s = pT[0][:, 0]

        bank = [[ctx.enter_context(nc.psum_tensor(f"bank{s}{b}", [P, 2, 256], F32)) for b in range(4)]
                for s in range(SLOTS)]

        sems = {n: [ctx.enter_context(nc.semaphore(f"{n}{s}")) for s in range(SLOTS)] for n in PER_GRAPH}
        weights_loaded = ctx.enter_context(nc.semaphore("weights_loaded"))
        consts_set = ctx.enter_context(nc.semaphore("consts_set"))
        zeros_set = ctx.enter_context(nc.semaphore("zeros_set"))
        eye_ready = ctx.enter_context(nc.semaphore("eye_ready"))
        wait_carried = ctx.enter_context(nc.semaphore("wait_carried"))
        wa_psum = ctx.enter_context(nc.semaphore("wa_psum"))
        wa_ready = ctx.enter_context(nc.semaphore("wa_ready"))

        def row(name):
            return rows_s[:, ROWS.index(name), :]

        def rowt(name):
            r = ROWS.index(name)
            return rows_s[:, r:r + 1, :].broadcast_to([P, NT, D])

        def col(name, k):
            c = COLS[name][0] + k
            return cols_s[:, c:c + 1]

        def sem(name, s):
            return sems[name][s]

        def nth(name, i, k):
            return i * PER_GRAPH[name] + (k if name in PRIMED else k - PER_GRAPH[name])

        def past(name, i):
            assert name in PRIMED
            return i * PER_GRAPH[name]

        def head_window(s, layer, h, t):
            if layer == 2:
                a = h * P + 64 - HO * (h % 2)
                return vp2[s][:, t, a:a + P]
            a = h * P + 96 - HD * (h % 4)
            return vp[s][:, t, a:a + P]

        def attention(layer):
            n = ATTN[layer][1]
            if layer == 2:
                yield "edges", layer, 0
            for k in range(n + 2):
                if layer == 2 and k + 1 < n:
                    yield "edges", layer, k + 1
                if k == n + 1:
                    yield "spread", layer
                for what in ATTN_ORDER[layer]:
                    if 0 <= k - HEADS_BEHIND[what] < n:
                        yield what, layer, k - HEADS_BEHIND[what]
                if k == n:
                    yield "widen", layer
                if layer == 3 and k == AHEAD_OF_NEXT:
                    yield "next", "prepare"
                    yield "next", "stats", PRE0
                if layer == 3 and k == AHEAD_OF_NEXT + 1:
                    yield "next", "scale", PRE0
            yield "normal", layer

        def normed(ln):
            return ("stats", ln), ("scale", ln)

        START = [("prepare",), *normed(PRE0)]
        FIRST = [("adj_turn",), ("norm", PRE0), ("relu", PRE0), ("masks",), ("qk", 0), ("v", 0), *attention(0), ("attn_out", 0),
                 ("attn_add", 0), *normed(POST1), ("norm", POST1), ("relu", POST1), *(("ff1", f) for f in range(4)), ("ff2", 0), ("ff2", 1), ("ff_add",),
                 *normed(POST2)]
        SECOND = [("gain0",), ("add0",), *normed(PRE1), ("norm", PRE1), ("relu", PRE1), ("mean_in",), ("mean_out",),
                  ("mean_add",), *normed(PRE2), ("norm", PRE2), ("relu", PRE2), ("types_in",), *attention(2),
                  ("types_out",), ("types_add",), ("types_mean",), ("types_center",), ("types_scale",),
                  ("types_gain",), ("types_end",), *normed(PRE3), ("norm", PRE3), ("relu", PRE3), ("qk", 3), ("v", 3),
                  *attention(3), ("attn_out", 3), ("attn_add", 3)]

        def beside(one_half, s1, ahead1, other_half, s2, ahead2):
            def starts(half):
                lengths = [LENGTH.get(step[:2], LENGTH.get(step[:1], 0)) for step in half]
                return [sum(lengths[:k]) / sum(lengths) for k in range(len(half))]

            both = [(at, 0, k, s1, ahead1, *step) for k, (at, step) in enumerate(zip(starts(one_half), one_half))]
            both += [(at, 1, k, s2, ahead2, *step) for k, (at, step) in enumerate(zip(starts(other_half), other_half))]
            both.sort(key=lambda step: step[:3])
            return [(s, ahead + 1, *step[1:]) if step[0] == "next" else (s, ahead, *step)
                    for _, _, _, s, ahead, *step in both]

        LAST = [step for step in SECOND if step[0] != "next"]
        OPENING = [(1, 0, *step) for step in START] + [(0, 0, *step) for step in START] + [(1, 0, *step) for step in FIRST]
        ROUND = beside(FIRST, 0, 0, SECOND, 1, 0) + beside(SECOND, 0, 0, FIRST, 1, 1)
        CLOSING = beside(FIRST, 0, 0, LAST, 1, 0) + [(0, 0, *step) for step in LAST]

        ln_src = {PRE0: ("x_loaded", 16, xin), POST1: ("r1_ready", 1, r1), POST2: ("r2_ready", 1, r1),
                  PRE1: ("xa_ready", 1, xa), PRE2: ("xb_ready", 1, xb), PRE3: ("xc_ready", 1, xc)}

        block = ctx.enter_context(nc.Block())

        @block.sync
        def _(sp):
            for name in PRIMED:
                for s in range(SLOTS):
                    sp.sem_inc(sem(name, s), PER_GRAPH[name])
            for dst, src in ((wqkv0_s, wqkv0), (wo0_s, wo0), (w1_s, w1), (w2_s, w2), (wl1_s, wl1),
                             (w2t_s, w2t), (ablk_s, ablk), (wqkv3_s, wqkv3), (wo3_s, wo3)):
                sp.dma_start(dst[:] if dst is not w2t_s else dst, src.rearrange("(t p) n -> p t n", p=P)).then_inc(weights_loaded, 16)
            sp.dma_start(wl2_s[:, :, 0:D], wl2.rearrange("(t p) n -> p t n", p=P)).then_inc(weights_loaded, 16)
            sp.dma_start(rows_s[:], rows).then_inc(weights_loaded, 16)
            sp.dma_start(cols_s[:], cols).then_inc(weights_loaded, 16)

            def load(s, i):
                sp.wait_ge(sem("adjf_ready", s), past("adjf_ready", i))
                sp.sem_inc(wait_carried, 1)
                sp.dma_start(adji[s][:], adj_v[i * SLOTS + (s - SLOTS)]).then_inc(sem("adj_loaded", s), 16)
                sp.wait_ge(sem("xplus", s), past("xplus", i))
                sp.sem_inc(wait_carried, 1)
                sp.wait_ge(sem("ln_z", s), past("ln_z", i))
                sp.sem_inc(wait_carried, 1)
                sp.dma_start(xin[s][:], x_v[i * SLOTS + (s - SLOTS)]).then_inc(sem("x_loaded", s), 16)

            def store(s, i):
                sp.wait_ge(sem("out_ready", s), nth("out_ready", i, 1))
                sp.sem_inc(wait_carried, 1)
                sp.dma_start(out_v[i * SLOTS + (s - SLOTS)], xo[s][:]).then_inc(sem("out_stored", s), 16)

            load(1, 1)
            load(0, 1)
            with sp.Fori(1, rounds) as i:
                load(1, i + 1)
                store(1, i)
                load(0, i + 1)
                store(0, i)
            store(1, rounds)
            store(0, rounds)
            for s in range(SLOTS):
                sp.wait_ge(sem("out_stored", s), 16 * (rounds + 1))

        @block.gpsimd
        def _(pool):
            nc.gpsimd.memset(power[:], -0.5).then_inc(consts_set, 1)
            nc.gpsimd.memset(ones[:], 1.0).then_inc(consts_set, 1)
            nc.gpsimd.memset(ident[:], 0.0).then_inc(consts_set, 1)
            nc.gpsimd.memset(identb[:], 0.0).then_inc(consts_set, 1)
            nc.gpsimd.memset(off_diagonal[:], MASKED).then_inc(consts_set, 1)
            pool.wait_ge(consts_set, 5)
            for m in (ident, identb):
                nc.gpsimd.affine_select(out=m[:], in_=m[:], compare_op=ALU.not_equal, fill=1.0, base=0,
                                        pattern=[[-1, P]], channel_multiplier=1).then_inc(eye_ready, 1)
            for t in range(NT):
                nc.gpsimd.affine_select(out=off_diagonal[:, t, :], in_=off_diagonal[:, t, :], compare_op=ALU.not_equal, fill=0.0,
                                        base=t * P, pattern=[[-1, N]], channel_multiplier=1).then_inc(eye_ready, 1)
            pool.wait_ge(weights_loaded, 16 * 12)
            nc.gpsimd.tensor_tensor(lnb2[:], row("ln1_b"), row("b2"), ALU.add).then_inc(eye_ready, 1)
            pool.wait_ge(eye_ready, 5)

            def powered(i, s, eps, src, tmp, dst, steps, done, n, k):
                nc.gpsimd.tensor_scalar(tmp, src, eps, None, ALU.add).then_inc(sem(steps, s), 1)
                pool.wait_ge(sem(steps, s), nth(steps, i, k + 1))
                pool.sem_inc(wait_carried, 1)
                nc.gpsimd.tensor_tensor(dst, tmp, power[:, 0:n], ALU.pow).then_inc(sem(done, s), 1)

            def go(steps, graph):
                for s, ahead, what, *arg in steps:
                    i = graph + ahead
                    if what == "stats":
                        ln = arg[0]
                        pool.wait_ge(sem("ln_aggr", s), nth("ln_aggr", i, 2 * ln + 2))
                        pool.sem_inc(wait_carried, 1)
                        powered(i, s, EPS_PRE, mv[s][:, :, 1], var[s][:], rstd[s][:], "ln_var", "ln_rstd", NT, ln)
                    if what == "scale":
                        ln = arg[0]
                        if ln == PRE0:
                            pool.wait_ge(sem("ln_z", s), nth("ln_z", i, 2))
                            pool.sem_inc(wait_carried, 1)
                            pool.wait_ge(sem("r1_ready", s), past("r1_ready", i))
                            pool.sem_inc(wait_carried, 1)
                            nc.gpsimd.tensor_scalar(hb[s][:], z[s][:], 0.0, None, ALU.max).then_inc(sem("hb_ready", s), 1)
                            pool.wait_ge(sem("hb_ready", s), nth("hb_ready", i, 1))
                            pool.sem_inc(wait_carried, 1)
                            nc.gpsimd.tensor_tensor(hb[s][:], hb[s][:], rowt("bo0"), ALU.add)\
                                .then_inc(sem("hb_ready", s), 1)
                        if ln == POST1:
                            pool.wait_ge(sem("ln_z", s), nth("ln_z", i, 4))
                            pool.sem_inc(wait_carried, 1)
                            pool.wait_ge(sem("r2_ready", s), past("r2_ready", i))
                            pool.sem_inc(wait_carried, 1)
                            nc.gpsimd.tensor_tensor(r1n[s][:], z[s][:], rowt("ln1_g"), ALU.mult)\
                                .then_inc(sem("r1n_ready", s), 1)
                            pool.wait_ge(sem("r1n_ready", s), nth("r1n_ready", i, 1))
                            pool.sem_inc(wait_carried, 1)
                            nc.gpsimd.tensor_tensor(r1n[s][:], r1n[s][:], lnb2[:, None, :].broadcast_to([P, NT, D]), ALU.add)\
                                .then_inc(sem("r1n_ready", s), 1)
                    if what == "masks":
                        pool.wait_ge(sem("adjf_ready", s), nth("adjf_ready", i, 1))
                        pool.sem_inc(wait_carried, 1)
                        pool.wait_ge(sem("beyond_col", s), past("beyond_col", i))
                        pool.sem_inc(wait_carried, 1)
                        nc.gpsimd.tensor_scalar(beyond[s][:], adjf[s][:], -1.0, None, ALU.add)\
                            .then_inc(sem("beyond_step", s), 1)
                        pool.wait_ge(sem("beyond_step", s), nth("beyond_step", i, 1))
                        pool.sem_inc(wait_carried, 1)
                        nc.gpsimd.tensor_tensor(beyond[s][:], beyond[s][:], adjf[s][:], ALU.mult)\
                            .then_inc(sem("beyond_step", s), 1)
                        pool.wait_ge(sem("xa_ready", s), past("xa_ready", i))
                        pool.sem_inc(wait_carried, 1)
                        nc.gpsimd.tensor_tensor(xplus[s][:], xin[s][:], rowt("ln2_b"), ALU.add)\
                            .then_inc(sem("xplus", s), 1)
                    if what == "types_in":
                        pool.wait_ge(sem("ln_z", s), nth("ln_z", i, 10))
                        pool.sem_inc(wait_carried, 1)
                        nc.gpsimd.tensor_tensor(xb[s][:], xb[s][:], rowt("l2_b"), ALU.add).then_inc(sem("x_bias", s), 1)
                    if what == "types_mean":
                        pool.wait_ge(sem("hln_aggr", s), nth("hln_aggr", i, 8))
                        pool.sem_inc(wait_carried, 1)
                        powered(i, s, EPS_L2, hmv[s][:, :, 1], hvar[s][:], hrs[s][:], "hln_var", "hln_rstd", 8, 0)
                    if what == "qk" and arg[0] == 3:
                        pool.wait_ge(sem("ln_z", s), nth("ln_z", i, 12))
                        pool.sem_inc(wait_carried, 1)
                        pool.wait_ge(sem("xc_ready", s), nth("xc_ready", i, 1))
                        pool.sem_inc(wait_carried, 1)
                        nc.gpsimd.tensor_tensor(xc[s][:], xc[s][:], rowt("bo3"), ALU.add).then_inc(sem("x_bias", s), 1)

            go(OPENING, 1)
            with pool.Fori(1, rounds) as i:
                go(ROUND, i)
            go(CLOSING, rounds)

        @block.scalar
        def _(act):
            act.wait_ge(weights_loaded, 16 * 12)
            act.wait_ge(wa_psum, 1)
            nc.scalar.activation(wl2_s[:, :, D:D + EC], bank[0][0][:, :, 0:EC], ACT.Copy).then_inc(wa_ready, 1)
            act.wait_ge(zeros_set, 6 * SLOTS)

            def go(steps, graph):
                for s, ahead, what, *arg in steps:
                    i = graph + ahead
                    b = bank[s]
                    if what == "prepare":
                        act.wait_ge(sem("adj_loaded", s), nth("adj_loaded", i, 16))
                        act.wait_ge(sem("msg_psum", s), past("msg_psum", i))
                        act.wait_ge(sem("adjT_psum", s), past("adjT_psum", i))
                        act.wait_ge(sem("others", s), past("others", i))
                        act.wait_ge(sem("beyond_step", s), past("beyond_step", i))
                        nc.scalar.activation(adjf[s][:], adji[s][:], ACT.Copy).then_inc(sem("adjf_ready", s), 1)
                    if what == "adj_turn":
                        act.wait_ge(sem("adjT_psum", s), nth("adjT_psum", i, 1))
                        act.wait_ge(sem("others", s), past("others", i))
                        act.wait_ge(sem("one_ready", s), past("one_ready", i))
                        act.wait_ge(sem("mask2_ready", s), past("mask2_ready", i))
                        nc.scalar.activation(adjT[s][:], b[1][:], ACT.Copy).then_inc(sem("adjT_ready", s), 1)
                    if what == "relu":
                        ln = arg[0]
                        act.wait_ge(sem("zT_psum", s), nth("zT_psum", i, TRANSPOSED[ln] + 1))
                        if ln == POST1:
                            for k in range(KT):
                                nc.scalar.activation(hT[s][:, k, :], b[2][:, k, :], ACT.Identity,
                                   bias=col("ln1_b", k), scale=col("ln1_g", k)).then_inc(sem("hT_ready", s), 1)
                        else:
                            nc.scalar.activation(hT[s][:], b[2][:], ACT.Relu).then_inc(sem("hT_ready", s), 1)
                    if what == "qk":
                        act.wait_ge(sem("qk_psum", s), nth("qk_psum", i, 2 + 2 * (arg[0] == 3)))
                        if arg[0] == 0:
                            act.wait_ge(sem("s_psum", s), past("s_psum", i))
                            for k in range(2):
                                nc.scalar.activation(kT[s][:, k, :], b[1][:, k, :], ACT.Identity, bias=col("bk", k)).then_inc(sem("k_ready", s), 1)
                        else:
                            nc.scalar.activation(kT[s][:], b[1][:], ACT.Copy).then_inc(sem("k_ready", s), 1)
                    if what == "v":
                        if arg[0] == 3:
                            act.wait_ge(sem("v_psum", s), nth("v_psum", i, 2))
                            for t in range(NT):
                                nc.scalar.activation(vp[s][:, t, 96:VW].rearrange("p (h c) -> p h c", c=P)[:, :, 0:HD],
                                   b[3][:, t, :].rearrange("p (h d) -> p h d", d=HD), ACT.Copy).then_inc(sem("v_ready", s), 1)
                    if what == "exp":
                        layer, h = arg
                        a = ATTN[layer][0] + h
                        act.wait_ge(sem("negmax", s), nth("negmax", i, a + 1))
                        if layer == 2:
                            act.wait_ge(sem("z_leaky", s), nth("z_leaky", i, h + 1))
                        if a >= 2:
                            act.wait_ge(sem("pT_psum", s), nth("pT_psum", i, a - 1))
                        src = zl[s][a % 2][:] if layer == 2 else b[a % 2]
                        for t in range(NT):
                            nc.scalar.activation(pr[s][:, a % 2, t, :], src[:, t, :], ACT.Exp,
                               bias=nmax[s][:, a % 2, t:t + 1], accum_out=rsum[s][:, t, h:h + 1]).then_inc(sem("probs", s), 1)
                    if what == "move":
                        layer, h = arg
                        a = ATTN[layer][0] + h
                        act.wait_ge(sem("pT_psum", s), nth("pT_psum", i, a + 1))
                        if a >= 2:
                            act.wait_ge(sem("pv_done", s), nth("pv_done", i, a - 1))
                        nc.scalar.activation(pT[s][:, a % 2], b[2][:], ACT.Copy).then_inc(sem("pT_ready", s), 1)
                    if what == "spread":
                        n = ATTN_NO[arg[0]]
                        act.wait_ge(sem("rT_psum", s), nth("rT_psum", i, n + 1))
                        nc.scalar.activation(rT[s][:], b[2][:], ACT.Copy).then_inc(sem("rT_ready", s), 1)
                    if what == "ff1" and arg[0] % 2 == 0:
                        f = arg[0]
                        act.wait_ge(sem("ff1_psum", s), nth("ff1_psum", i, f + 1))
                        for k in range(2):
                                nc.scalar.activation(ffT[s][:, 2 * f + k, :], b[f % 2][:, k, :], ACT.Relu,
                                   bias=col("b1", 2 * f + k)).then_inc(sem("ff_act", s), 1)
                    if what == "mean_in":
                        for t in range(NT):
                            act.wait_ge(sem("l1_psum", s), nth("l1_psum", i, t + 1))
                            nc.scalar.activation(hm[s][:, t, 0:D], b[t][:, 0, :], ACT.Copy).then_inc(sem("hm_ready", s), 1)
                    if what == "types_in":
                        for t in range(NT):
                            act.wait_ge(sem("l2_psum", s), nth("l2_psum", i, t + 1))
                            nc.scalar.activation(vp2[s][:, t, 64:VW2].rearrange("p (h c) -> p h c", c=P)[:, :, 0:HO],
                               b[t][:, 0, :].rearrange("p (h d) -> p h d", d=HO), ACT.Copy).then_inc(sem("h2_ready", s), 1)
                    if what == "types_out":
                        for k in range(KT):
                            act.wait_ge(sem("ctxT_ready", s), nth("ctxT_ready", i, 3 + k))
                            nc.scalar.activation(rT[s][:, k, :], ctxT[s][:, k, :], ACT.Relu, bias=col("l2_bias", k)).then_inc(sem("c2_ready", s), 1)

            go(OPENING, 1)
            with act.Fori(1, rounds) as i:
                go(ROUND, i)
            go(CLOSING, rounds)

        @block.tensor
        def _(pe):
            def mm(o, lhsT, rhs, start, stop, **k):
                return nc.tensor.matmul(o, lhsT, rhs, start=start, stop=stop, **k)

            pe.wait_ge(weights_loaded, 16 * 12)
            pe.wait_ge(eye_ready, 4)
            for d in range(KT):
                for k in range(KT):
                    m = mm(bank[0][0][:, d, 0:EC], w2t_s[:, k, d * P:(d + 1) * P], ablk_s[:, k, :], k == 0, k == KT - 1)
            m.then_inc(wa_psum, 1)
            pe.wait_ge(wa_ready, 1)
            pe.wait_ge(zeros_set, 6 * SLOTS)

            def go(steps, graph):
                for s, ahead, what, *arg in steps:
                    i = graph + ahead
                    b = bank[s]
                    if what == "adj_turn":
                        pe.wait_ge(sem("adjf_ready", s), nth("adjf_ready", i, 1))
                        pe.wait_ge(sem("probs", s), past("probs", i))
                        for k in range(NT):
                            for t in range(NT):
                                m = nc.tensor.transpose(b[1][:, k, t * P:(t + 1) * P], adjf[s][:, t, k * P:(k + 1) * P],
                                                        ident[:])
                        m.then_inc(sem("adjT_psum", s), 1)
                    if what == "norm":
                        for t in range(NT):
                            pe.wait_ge(sem("ln_z", s), nth("ln_z", i, 2 * arg[0] + t + 1))
                            for k in range(KT):
                                m = nc.tensor.transpose(b[2][:, k, t * P:(t + 1) * P], z[s][:, t, k * P:(k + 1) * P],
                                                        ident[:])
                        m.then_inc(sem("zT_psum", s), 1)
                    if what == "qk":
                        layer = arg[0]
                        w = wqkv0_s if layer == 0 else wqkv3_s
                        pe.wait_ge(sem("hT_ready", s), nth("hT_ready", i, HT_DONE[PRE0 if layer == 0 else PRE3]))
                        if layer == 0:
                            pe.wait_ge(sem("adjT_ready", s), nth("adjT_ready", i, 1))
                            pe.wait_ge(sem("ln_z", s), nth("ln_z", i, 2))
                            pe.wait_ge(sem("out_ready", s), past("out_ready", i))
                        else:
                            pe.wait_ge(sem("o2_ready", s), nth("o2_ready", i, 1))
                        for part in range(2):
                            for g in range(2):
                                c = part * D + g * P
                                for k in range(KT):
                                    m = mm(b[part][:, g, :], w[:, k, c:c + P], hT[s][:, k, :], k == 0, k == KT - 1)
                            m.then_inc(sem("qk_psum", s), 1)
                    if what == "v":
                        w = wqkv0_s if arg[0] == 0 else wqkv3_s
                        for t in range(NT):
                            for k in range(KT):
                                m = mm(b[3][:, t, :], hT[s][:, k, t * P:(t + 1) * P], w[:, k, 2 * D:3 * D],
                                       k == 0, k == KT - 1)
                        m.then_inc(sem("v_psum", s), 1)
                    if what == "scores":
                        layer, h = arg
                        a = ATTN[layer][0] + h
                        if layer == 2:
                            pe.wait_ge(sem("uw", s), nth("uw", i, 4 * (h + 1)))
                            pe.wait_ge(sem("others", s), nth("others", i, OTHERS * (h + 1)))
                            if h >= 2:
                                pe.wait_ge(sem("z_sum", s), nth("z_sum", i, h - 1))
                            for t in range(NT):
                                for j in range(NT):
                                    m = nc.tensor.transpose(b[a % 2][:, t, j * P:(j + 1) * P],
                                                            ww[s][:, h % 2, j, t * P:(t + 1) * P], ident[:])
                        else:
                            qk = 2 if layer == 0 else 3
                            pe.wait_ge(sem("q_ready", s), nth("q_ready", i, qk))
                            pe.wait_ge(sem("k_ready", s), nth("k_ready", i, qk))
                            if h == 0:
                                if layer == 0:
                                    pe.wait_ge(sem("mask0_ready", s), nth("mask0_ready", i, 1))
                                else:
                                    pe.wait_ge(sem("mask3_ready", s), nth("mask3_ready", i, 1))
                            if h >= 2:
                                pe.wait_ge(sem("probs", s), nth("probs", i, 2 * (a - 1)))
                            g, r = h // 4, HD * (h % 4)
                            mask = mask0[s] if layer == 0 else mask3[s]
                            for t in range(NT):
                                mm(b[a % 2][:, t, :], identb[:], mask[:, t, :], True, False)
                                m = mm(b[a % 2][:, t, :], qT[s][r:r + HD, g, t * P:(t + 1) * P], kT[s][r:r + HD, g, :],
                                       False, True)
                        m.then_inc(sem("s_psum", s), 1)
                    if what == "turn":
                        layer, h = arg
                        a = ATTN[layer][0] + h
                        if a:
                            pe.wait_ge(sem("pT_ready", s), nth("pT_ready", i, a))
                        for t in range(NT):
                            pe.wait_ge(sem("probs", s), nth("probs", i, 2 * a + t + 1))
                            for j in range(NT):
                                m = nc.tensor.transpose(b[2][:, j, t * P:(t + 1) * P],
                                                        pr[s][:, a % 2, t, j * P:(j + 1) * P], ident[:])
                        m.then_inc(sem("pT_psum", s), 1)
                    if what == "weigh":
                        layer, h = arg
                        a = ATTN[layer][0] + h
                        per = 2 if layer == 2 else 4
                        pe.wait_ge(sem("pT_ready", s), nth("pT_ready", i, a + 1))
                        if h == 0:
                            if layer == 2:
                                pe.wait_ge(sem("h2_ready", s), nth("h2_ready", i, 2))
                            else:
                                pe.wait_ge(sem("v_ready", s), nth("v_ready", i, 2 + 2 * (layer == 3)))
                        for j in range(NT):
                            m = mm(b[3][:, h // per, :], head_window(s, layer, h, j), pT[s][:, a % 2, j, :],
                                   h % per == 0 and j == 0, h % per == per - 1 and j == NT - 1)
                        m.then_inc(sem("pv_done", s), 1)
                    if what == "spread":
                        n = ATTN_NO[arg[0]]
                        pe.wait_ge(sem("rwide", s), nth("rwide", i, n + 1))
                        first, heads = ATTN[arg[0]]
                        pe.wait_ge(sem("pT_ready", s), nth("pT_ready", i, first + heads))
                        for k in range(KT):
                            for t in range(NT):
                                m = nc.tensor.transpose(b[2][:, k, t * P:(t + 1) * P],
                                                        rwide[s][:, t, k * P:(k + 1) * P], ident[:])
                        m.then_inc(sem("rT_psum", s), 1)
                    if what == "attn_out":
                        w = wo0_s if arg[0] == 0 else wo3_s
                        for t in range(NT):
                            for k in range(KT):
                                if t == 0:
                                    pe.wait_ge(sem("ctxT_ready", s), nth("ctxT_ready", i, 2 * ATTN_NO[arg[0]] + k + 1))
                                m = mm(b[0][:, t, :], ctxT[s][:, k, t * P:(t + 1) * P], w[:, k, :], k == 0, k == KT - 1)
                        m.then_inc(sem("wo_psum", s), 1)
                    if what == "ff1":
                        f = arg[0]
                        if f == 0:
                            pe.wait_ge(sem("hT_ready", s), nth("hT_ready", i, HT_DONE[POST1]))
                        if f == 2:
                            pe.wait_ge(sem("ff_act", s), nth("ff_act", i, 2))
                        if f == 3:
                            pe.wait_ge(sem("ff_dve", s), nth("ff_dve", i, 2))
                        for u in range(2):
                            c = (2 * f + u) * P
                            for k in range(KT):
                                m = mm(b[f % 2][:, u, :], w1_s[:, k, c:c + P], hT[s][:, k, :], k == 0, k == KT - 1)
                        m.then_inc(sem("ff1_psum", s), 1)
                    if what == "ff2":
                        t = arg[0]
                        for f in range(FT):
                            if t == 0 and f % 4 == 0:
                                pe.wait_ge(sem("ff_act", s), nth("ff_act", i, f // 2 + 2))
                            if t == 0 and f % 4 == 2:
                                pe.wait_ge(sem("ff_dve", s), nth("ff_dve", i, f // 2 + 1))
                            m = mm(b[3][:, t, :], ffT[s][:, f, t * P:(t + 1) * P], w2_s[:, f, :], f == 0, f == FT - 1)
                        m.then_inc(sem("ff2_psum", s), 1)
                    if what == "mean_in":
                        pe.wait_ge(sem("hT_ready", s), nth("hT_ready", i, HT_DONE[PRE1]))
                        for t in range(NT):
                            for k in range(KT):
                                m = mm(b[t][:].rearrange("p a c -> p (a c)"), hT[s][:, k, t * P:(t + 1) * P],
                                       wl1_s[:, k, :], k == 0, k == KT - 1)
                            m.then_inc(sem("l1_psum", s), 1)
                    if what == "mean_out":
                        for j in range(NT):
                            o = b[2 + j][:].rearrange("p a c -> p (a c)")[:, 0:D + 1]
                            for t in range(NT):
                                if j == 0:
                                    pe.wait_ge(sem("hm_ready", s), nth("hm_ready", i, t + 1))
                                m = mm(o, adjf[s][:, t, j * P:(j + 1) * P], hm[s][:, t, :], t == 0, t == NT - 1)
                            m.then_inc(sem("msg_psum", s), 1)
                    if what == "types_in":
                        pe.wait_ge(sem("hT_ready", s), nth("hT_ready", i, HT_DONE[PRE2]))
                        pe.wait_ge(sem("beyond_col", s), nth("beyond_col", i, 1))
                        mm(b[1][:, 1, N - 1:N], ones[:], beyond_col[s][:], True, True).then_inc(sem("beyond_psum", s), 1)
                        for t in range(NT):
                            for k in range(KT):
                                m = mm(b[t][:].rearrange("p a c -> p (a c)")[:, 0:D + EC],
                                       hT[s][:, k, t * P:(t + 1) * P], wl2_s[:, k, :], k == 0, k == KT - 1)
                            m.then_inc(sem("l2_psum", s), 1)
                    if what == "types_out":
                        for k in range(KT):
                            pe.wait_ge(sem("c2_ready", s), nth("c2_ready", i, k + 1))
                            for t in range(NT):
                                m = nc.tensor.transpose(b[0][:, t, k * P:(k + 1) * P], rT[s][:, k, t * P:(t + 1) * P],
                                                        ident[:])
                        m.then_inc(sem("c2_psum", s), 1)

            go(OPENING, 1)
            with pe.Fori(1, rounds) as i:
                go(ROUND, i)
            go(CLOSING, rounds)

        @block.vector
        def _(dve):
            V = nc.vector
            for s in range(SLOTS):
                for t in range(NT):
                    V.memset(vp[s][:, t, :], 0.0).then_inc(zeros_set, 1)
                    V.memset(vp2[s][:, t, :], 0.0).then_inc(zeros_set, 1)
                    V.memset(hm[s][:, t, D:D + 1], 1.0).then_inc(zeros_set, 1)
            dve.wait_ge(zeros_set, 6 * SLOTS)
            dve.wait_ge(weights_loaded, 16 * 12)
            dve.wait_ge(eye_ready, 5)

            def go(steps, graph):
                for s, ahead, what, *arg in steps:
                    i = graph + ahead
                    b = bank[s]
                    if what == "stats":
                        ln = arg[0]
                        name, k, src = ln_src[ln]
                        dve.wait_ge(sem(name, s), nth(name, i, k))
                        for t in range(NT):
                            V.bn_stats(st[s][:, t, :], src[s][:, t, :]).then_inc(sem("ln_stats", s), 1)
                        dve.wait_ge(sem("ln_stats", s), nth("ln_stats", i, 2 * ln + 2))
                        dve.sem_inc(wait_carried, 1)
                        for t in range(NT):
                            V.bn_aggr(mv[s][:, t, :], st[s][:, t, :]).then_inc(sem("ln_aggr", s), 1)
                    if what == "scale":
                        ln = arg[0]
                        src = ln_src[ln][2]
                        dve.wait_ge(sem("ln_rstd", s), nth("ln_rstd", i, ln + 1))
                        for t in range(NT):
                            V.tensor_scalar(z[s][:, t, :], src[s][:, t, :], mv[s][:, t, 0:1], rstd[s][:, t:t + 1],
                                            ALU.subtract, ALU.mult).then_inc(sem("ln_z", s), 1)
                    if what == "masks":
                        dve.wait_ge(sem("adjT_ready", s), nth("adjT_ready", i, 1))
                        V.tensor_tensor(mtmp[s][:], adjf[s][:], adjT[s][:], ALU.max).then_inc(sem("mask0_step", s), 1)
                        dve.wait_ge(sem("mask0_step", s), nth("mask0_step", i, 1))
                        V.scalar_tensor_tensor(mask0[s][:], mtmp[s][:], 0.0, off_diagonal[:], ALU.is_le, ALU.mult)\
                            .then_inc(sem("mask0_ready", s), 1)
                    if what == "qk":
                        layer = arg[0]
                        dve.wait_ge(sem("qk_psum", s), nth("qk_psum", i, 1 + 2 * (layer == 3)))
                        if layer == 0:
                            for k in range(2):
                                V.tensor_scalar(qT[s][:, k, :], b[0][:, k, :], col("bq", k), QSCALE, ALU.add, ALU.mult)\
                                    .then_inc(sem("q_ready", s), 1)
                        else:
                            V.tensor_scalar(qT[s][:], b[0][:], QSCALE, None, ALU.mult).then_inc(sem("q_ready", s), 1)
                    if what == "v" and arg[0] == 0:
                        dve.wait_ge(sem("v_psum", s), nth("v_psum", i, 1))
                        for t in range(NT):
                            V.tensor_tensor(vp[s][:, t, 96:VW].rearrange("p (h c) -> p h c", c=P)[:, :, 0:HD],
                                            b[3][:, t, :].rearrange("p (h d) -> p h d", d=HD),
                                            row("bv").rearrange("p (h d) -> p h d", d=HD), ALU.add)\
                                .then_inc(sem("v_ready", s), 1)
                    if what == "edges":
                        layer, h = arg
                        if h == 0:
                            dve.wait_ge(sem("one_ready", s), nth("one_ready", i, 2))
                            dve.wait_ge(sem("e_ready", s), nth("e_ready", i, 2))
                        src_col, dst_col = h * TYPES, (H2 + h) * TYPES
                        for n in range(NT):
                            V.scalar_tensor_tensor(ww[s][:, h % 2, n, :], oneT[s][:, n, :],
                                                   esd[s][:, n, dst_col:dst_col + 1], mask2[s][:, n, :],
                                                   ALU.mult, ALU.add).then_inc(sem("uw", s), 1)
                            V.tensor_scalar(uu[s][:, h % 2, n, :], one[s][:, n, :],
                                            esd[s][:, n, src_col:src_col + 1], None, ALU.mult)\
                                .then_inc(sem("uw", s), 1)
                        if h == 0:
                            dve.wait_ge(sem("beyond_flag", s), nth("beyond_flag", i, 1))
                            dve.sem_inc(wait_carried, 1)
                        has_others = dve.value_load(beyond_flag[s][0:1, 0:1])
                        with dve.If(has_others):
                            for t in range(1, TYPES):
                                k = OTHERS * h + 6 * (t - 1)
                                dve.wait_ge(sem("others", s), nth("others", i, k))
                                V.tensor_scalar(other[:], adjf[s][:], float(t + 1), None, ALU.is_equal)\
                                    .then_inc(sem("others", s), 1)
                                V.tensor_scalar(otherT[:], adjT[s][:], float(t + 1), None, ALU.is_equal)\
                                    .then_inc(sem("others", s), 1)
                                dve.wait_ge(sem("others", s), nth("others", i, k + 2))
                                dve.wait_ge(sem("uw", s), nth("uw", i, 4 * (h + 1)))
                                for n in range(NT):
                                    V.scalar_tensor_tensor(ww[s][:, h % 2, n, :], otherT[:, n, :],
                                                           esd[s][:, n, dst_col + t:dst_col + t + 1],
                                                           ww[s][:, h % 2, n, :],
                                                           ALU.mult, ALU.add).then_inc(sem("others", s), 1)
                                    V.scalar_tensor_tensor(uu[s][:, h % 2, n, :], other[:, n, :],
                                                           esd[s][:, n, src_col + t:src_col + t + 1],
                                                           uu[s][:, h % 2, n, :],
                                                           ALU.mult, ALU.add).then_inc(sem("others", s), 1)
                        with dve.Else():
                            dve.sem_inc(sem("others", s), OTHERS)
                    if what == "top":
                        layer, h = arg
                        a = ATTN[layer][0] + h
                        src = b[a % 2]
                        if layer == 2:
                            dve.wait_ge(sem("s_psum", s), nth("s_psum", i, a + 1))
                            dve.wait_ge(sem("uw", s), nth("uw", i, 4 * (h + 1)))
                            V.tensor_tensor(zs[s][:], src[:], uu[s][:, h % 2], ALU.add).then_inc(sem("z_sum", s), 1)
                            dve.wait_ge(sem("z_sum", s), nth("z_sum", i, h + 1))
                            V.scalar_tensor_tensor(zl[s][a % 2][:], zs[s][:], 0.01, zs[s][:], ALU.mult, ALU.max)\
                                .then_inc(sem("z_leaky", s), 1)
                            dve.wait_ge(sem("z_leaky", s), nth("z_leaky", i, h + 1))
                            src = zl[s][a % 2][:]
                        else:
                            dve.wait_ge(sem("s_psum", s), nth("s_psum", i, a + 1))
                        V.tensor_reduce(nmax[s][:, a % 2, :], src[:], AX.X, ALU.max, negate=True)\
                            .then_inc(sem("negmax", s), 1)
                    if what == "widen":
                        layer = arg[0]
                        n = ATTN_NO[layer]
                        first, heads = ATTN[layer]
                        dve.wait_ge(sem("probs", s), nth("probs", i, 2 * (first + heads)))
                        V.reciprocal(rinv[s][:, :, 0:heads], rsum[s][:, :, 0:heads]).then_inc(sem("rinv", s), 1)
                        dve.wait_ge(sem("rinv", s), nth("rinv", i, n + 1))
                        V.tensor_copy(rwide[s][:].rearrange("p t (h d) -> p t h d", h=heads),
                                      rinv[s][:, :, 0:heads, None].broadcast_to([P, NT, heads, D // heads]))\
                            .then_inc(sem("rwide", s), 1)
                    if what == "normal":
                        layer = arg[0]
                        n = ATTN_NO[layer]
                        first, heads = ATTN[layer]
                        dve.wait_ge(sem("rT_ready", s), nth("rT_ready", i, n + 1))
                        dve.wait_ge(sem("pv_done", s), nth("pv_done", i, first + heads))
                        for k in range(KT):
                            V.tensor_tensor(ctxT[s][:, k, :], b[3][:, k, :], rT[s][:, k, :], ALU.mult)\
                                .then_inc(sem("ctxT_ready", s), 1)
                    if what == "attn_add":
                        if arg[0] == 0:
                            dve.wait_ge(sem("wo_psum", s), nth("wo_psum", i, 1))
                            dve.wait_ge(sem("hb_ready", s), nth("hb_ready", i, 2))
                            V.tensor_tensor(r1[s][:], b[0][:], hb[s][:], ALU.add).then_inc(sem("r1_ready", s), 1)
                        else:
                            dve.wait_ge(sem("wo_psum", s), nth("wo_psum", i, 2))
                            dve.wait_ge(sem("x_bias", s), nth("x_bias", i, 2))
                            dve.wait_ge(sem("out_stored", s), past("out_stored", i))
                            V.tensor_tensor(xo[s][:], b[0][:], xc[s][:], ALU.add).then_inc(sem("out_ready", s), 1)
                    if what == "ff1" and arg[0] == 0:
                        V.tensor_scalar(mask3[s][:], adjf[s][:], 0.0, MASKED, ALU.is_le, ALU.mult)\
                            .then_inc(sem("mask3_ready", s), 1)
                        V.tensor_scalar(mask2[s][:], adjT[s][:], 0.0, MASKED, ALU.is_equal, ALU.mult)\
                            .then_inc(sem("mask2_ready", s), 1)
                    if what == "ff1" and arg[0] == 2:
                        V.tensor_scalar(one[s][:], adjf[s][:], 1.0, None, ALU.is_equal).then_inc(sem("one_ready", s), 1)
                        V.tensor_scalar(oneT[s][:], adjT[s][:], 1.0, None, ALU.is_equal).then_inc(sem("one_ready", s), 1)
                        dve.wait_ge(sem("beyond_step", s), nth("beyond_step", i, 2))
                        V.tensor_reduce(beyond_col[s][:], beyond[s][:], AX.XY, ALU.max).then_inc(sem("beyond_col", s), 1)
                    if what == "ff1" and arg[0] % 2 == 1:
                        f = arg[0]
                        dve.wait_ge(sem("ff1_psum", s), nth("ff1_psum", i, f + 1))
                        for k in range(2):
                            V.tensor_scalar(ffT[s][:, 2 * f + k, :], b[f % 2][:, k, :], col("b1", 2 * f + k), 0.0,
                                            ALU.add, ALU.max).then_inc(sem("ff_dve", s), 1)
                    if what == "ff_add":
                        dve.wait_ge(sem("ff2_psum", s), nth("ff2_psum", i, 2))
                        dve.wait_ge(sem("r1n_ready", s), nth("r1n_ready", i, 2))
                        V.tensor_tensor(r1[s][:], b[3][:], r1n[s][:], ALU.add).then_inc(sem("r2_ready", s), 1)
                    if what == "mean_in":
                        for t in range(NT):
                            dve.wait_ge(sem("l1_psum", s), nth("l1_psum", i, t + 1))
                            dve.wait_ge(sem("hm_ready", s), nth("hm_ready", i, t + 1))
                            V.tensor_tensor(upd[s][:, t, :], b[t][:, 1, :], row("l1_bias"), ALU.add)\
                                .then_inc(sem("upd_ready", s), 1)
                    if what == "mean_out":
                        for j in range(NT):
                            dve.wait_ge(sem("msg_psum", s), nth("msg_psum", i, j + 1))
                            dg = b[2 + j][:, 1, 0:1]
                            V.tensor_scalar(deg[s][:, j, 0:1], dg, 1.0, None, ALU.max).then_inc(sem("deg_step", s), 1)
                            dve.wait_ge(sem("deg_step", s), nth("deg_step", i, 3 * j + 1))
                            V.reciprocal(deg[s][:, j, 1:2], deg[s][:, j, 0:1]).then_inc(sem("deg_step", s), 1)
                            dve.wait_ge(sem("deg_step", s), nth("deg_step", i, 3 * j + 2))
                            V.scalar_tensor_tensor(deg[s][:, j, 2:3], dg, 0.0, deg[s][:, j, 1:2], ALU.is_gt, ALU.mult)\
                                .then_inc(sem("deg_step", s), 1)
                            dve.wait_ge(sem("deg_step", s), nth("deg_step", i, 3 * j + 3))
                            dve.wait_ge(sem("upd_ready", s), nth("upd_ready", i, j + 1))
                            V.scalar_tensor_tensor(upd[s][:, j, :], b[2 + j][:, 0, :], deg[s][:, j, 2:3], upd[s][:, j, :],
                                                   ALU.mult, ALU.add).then_inc(sem("msg_ready", s), 1)
                    if what == "mean_add":
                        dve.wait_ge(sem("msg_ready", s), nth("msg_ready", i, 2))
                        V.scalar_tensor_tensor(xb[s][:], upd[s][:], 0.0, xa[s][:], ALU.max, ALU.add)\
                            .then_inc(sem("xb_ready", s), 1)
                    if what == "types_in":
                        for t in range(NT):
                            dve.wait_ge(sem("h2_ready", s), nth("h2_ready", i, t + 1))
                            V.tensor_copy(esd[s][:, t, :], b[t][:, 1, 0:EC]).then_inc(sem("e_ready", s), 1)
                        dve.wait_ge(sem("beyond_psum", s), nth("beyond_psum", i, 1))
                        V.tensor_scalar(beyond_flag[s][:], b[1][:, 1, N - 1:N], 0.0, None, ALU.is_gt)\
                            .then_inc(sem("beyond_flag", s), 1)
                    if what == "types_add":
                        dve.wait_ge(sem("c2_psum", s), nth("c2_psum", i, 1))
                        V.tensor_tensor(o2[s][:].rearrange("p t (h d) -> p t h d", d=HO),
                                        b[0][:].rearrange("p t (h d) -> p t h d", d=HO),
                                        vp2[s][:, :, 64:VW2].rearrange("p t (h c) -> p t h c", c=P)[:, :, :, 0:HO],
                                        ALU.add).then_inc(sem("o2_ready", s), 1)
                    if what == "types_mean":
                        dve.wait_ge(sem("o2_ready", s), nth("o2_ready", i, 1))
                        oh = o2[s][:].rearrange("p t (h d) -> p (t h) d", d=HO)
                        for u in range(8):
                            V.bn_stats(hst[s][:, u, :], oh[:, u, :]).then_inc(sem("hln_stats", s), 1)
                        dve.wait_ge(sem("hln_stats", s), nth("hln_stats", i, 8))
                        dve.sem_inc(wait_carried, 1)
                        for u in range(8):
                            V.bn_aggr(hmv[s][:, u, :], hst[s][:, u, :]).then_inc(sem("hln_aggr", s), 1)
                    if what == "types_center":
                        oh = o2[s][:].rearrange("p t (h d) -> p (t h) d", d=HO)
                        dve.wait_ge(sem("hln_aggr", s), nth("hln_aggr", i, 8))
                        V.tensor_tensor(oh, oh, hmv[s][:, :, 0:1].broadcast_to([P, 8, HO]), ALU.subtract)\
                            .then_inc(sem("o2_step", s), 1)
                    if what == "types_scale":
                        oh = o2[s][:].rearrange("p t (h d) -> p (t h) d", d=HO)
                        dve.wait_ge(sem("o2_step", s), nth("o2_step", i, 1))
                        dve.wait_ge(sem("hln_rstd", s), nth("hln_rstd", i, 1))
                        V.tensor_tensor(oh, oh, hrs[s][:, :, None].broadcast_to([P, 8, HO]), ALU.mult)\
                            .then_inc(sem("o2_step", s), 1)
                    if what == "types_gain":
                        dve.wait_ge(sem("o2_step", s), nth("o2_step", i, 2))
                        dve.wait_ge(sem("x_bias", s), nth("x_bias", i, 1))
                        V.tensor_tensor(o2[s][:], o2[s][:], rowt("l2_g"), ALU.mult).then_inc(sem("gain_step", s), 1)
                    if what == "types_end":
                        dve.wait_ge(sem("gain_step", s), nth("gain_step", i, 2))
                        V.tensor_tensor(xc[s][:], o2[s][:], xb[s][:], ALU.add).then_inc(sem("xc_ready", s), 1)
                    if what == "gain0":
                        dve.wait_ge(sem("ln_z", s), nth("ln_z", i, 6))
                        V.tensor_tensor(r1[s][:], z[s][:], rowt("ln2_g"), ALU.mult).then_inc(sem("gain_step", s), 1)
                    if what == "add0":
                        dve.wait_ge(sem("gain_step", s), nth("gain_step", i, 1))
                        dve.wait_ge(sem("xplus", s), nth("xplus", i, 1))
                        V.tensor_tensor(xa[s][:], r1[s][:], xplus[s][:], ALU.add).then_inc(sem("xa_ready", s), 1)

            go(OPENING, 1)
            with dve.Fori(1, rounds) as i:
                go(ROUND, i)
            go(CLOSING, rounds)


def kernel(**inputs):
    import concourse.bacc as bacc
    from concourse.bass_utils import run_bass_kernel_spmd

    a = {n: np.asarray(v) for n, v in inputs.items()}
    d = np.float32

    def spread(v):
        return np.broadcast_to(np.asarray(v).reshape(1, D), (P, D))

    def columns(v):
        return np.asarray(v).reshape(-1, P).T

    rows = np.stack([spread(v) for v in (
        a["L0_gnn_bqkv"][2 * D:], a["L0_gnn_bo"], a["L0_gnn_ln1_g"], a["L0_gnn_ln1_b"], a["L0_gnn_b2"],
        a["L0_gnn_ln2_g"], a["L0_gnn_ln2_b"], a["L1_gnn_bias"], a["L2_gnn_ln_gamma"], a["L2_gnn_ln_beta"],
        a["L3_gnn_bo"])], axis=1)
    cols = np.concatenate([columns(v) for v in (
        a["L0_gnn_bqkv"][:D], a["L0_gnn_bqkv"][D:2 * D], a["L0_gnn_ln1_g"], a["L0_gnn_ln1_b"], a["L0_gnn_b1"],
        a["L2_gnn_bias"])], axis=1)
    ablk = np.zeros((D, 2, H2, TYPES), d)
    for h in range(H2):
        ablk[h * HO:(h + 1) * HO, 0, h] = a["L2_gnn_a_src"][h].T
        ablk[h * HO:(h + 1) * HO, 1, h] = a["L2_gnn_a_dst"][h].T
    arrays = {
        "x": a["x"], "adj": a["adj"],
        "wqkv0": a["L0_gnn_Wqkv"].T, "wo0": a["L0_gnn_Wo"].T, "w1": a["L0_gnn_W1"].T, "w2": a["L0_gnn_W2"].T,
        "wl1": np.concatenate([a["L1_gnn_W_msg"], a["L1_gnn_W_upd"]], axis=1),
        "wl2": a["L2_gnn_W"].transpose(1, 0, 2).reshape(D, D),
        "w2t": a["L2_gnn_W"].transpose(0, 2, 1).reshape(D, D),
        "ablk": ablk.reshape(D, 2 * H2 * TYPES),
        "wqkv3": np.concatenate([a["L3_gnn_Wq"], a["L3_gnn_Wk"], a["L3_gnn_Wv"]], axis=1),
        "wo3": a["L3_gnn_Wo"], "rows": rows, "cols": cols,
    }
    arrays = {n: np.ascontiguousarray(v) for n, v in arrays.items()}
    nc = bacc.Bacc("TRN2", target_bir_lowering=False, num_devices=1)
    args = [nc.dram_tensor(n, v.shape, mybir.dt.from_np(v.dtype), kind="ExternalInput").ap() for n, v in arrays.items()]
    out = nc.dram_tensor("out", a["x"].shape, F32, kind="ExternalOutput").ap()
    build(nc, *args, out)
    r = run_bass_kernel_spmd(nc, [arrays], core_ids=[0])
    return r.results[0]["out"]
```
